# Optimizing a Trainium2 kernel written in Bass

```python
import numpy as np
import jax
import jax.numpy as jnp

def _softmax(x, axis=-1):
    return jax.nn.softmax(x, axis=axis)

def _gelu(x):
    return jax.nn.gelu(x, approximate=True)

def _silu(x):
    return jax.nn.silu(x)

def _sigmoid(x):
    return jax.nn.sigmoid(x)

def _layernorm(x, axis=-1, eps=1e-05):
    m = jnp.mean(x, axis=axis, keepdims=True)
    v = jnp.var(x, axis=axis, keepdims=True)
    return (x - m) / jnp.sqrt(v + eps)

def _scatter_add(tgt, idx, src, axis=0):
    return tgt.at[idx].add(src)

def _segment_sum(src, seg, n):
    return jax.ops.segment_sum(src, seg, n)
kernel_name = 'mk_lm_tower_d1_tok_ids256_r4_f9e41c'

def setup_inputs(seed: int=0):
    np.random.seed(seed)
    _w = jnp.asarray

    def _rec_inputs():
        import jax
        import jax.numpy as jnp
        _rk = jax.random.key(seed)
        x = jax.random.randint(jax.random.fold_in(_rk, 1), (16, 128), 0, 64, jnp.int32)
        fside_BS_continuous_positions = jax.random.uniform(jax.random.fold_in(_rk, 21), (16, 128), jnp.float32, 0.0, 0.999927)
        return (x, fside_BS_continuous_positions)
    x, fside_BS_continuous_positions = _rec_inputs()

    def _L0_tok_setup():
        import jax, jax.numpy as jnp
        import numpy as np
        N_SCALES = 4

        def _conv1d(x, w, b, pad):
            y = jax.lax.conv_general_dilated(x, w, window_strides=(1,), padding=[(pad, pad)], dimension_numbers=('NCH', 'OIH', 'NCH'))
            return y + b[None, :, None]
        key = jax.random.key(seed)
        ks = jax.random.split(key, 12)
        B, S, P, D = (8, 512, 512, 64)
        byte_sequence = jax.random.randint(ks[0], (B, S), 0, 64, dtype=jnp.int64)
        continuous_positions = jax.random.uniform(ks[1], (B, P), dtype=jnp.float32)
        emb = jax.random.normal(ks[2], (64, D), dtype=jnp.float32)
        locality_shapes = jax.random.normal(ks[3], (64, 4), dtype=jnp.float32)
        w1 = jax.random.normal(ks[4], (128, 64, 7), dtype=jnp.float32) * 0.02
        b1 = jnp.zeros((128,), dtype=jnp.float32)
        w2 = jax.random.normal(ks[5], (64, 128, 5), dtype=jnp.float32) * 0.02
        b2 = jnp.zeros((64,), dtype=jnp.float32)
        w3 = jax.random.normal(ks[6], (1, 64, 3), dtype=jnp.float32) * 0.02
        b3 = jnp.zeros((1,), dtype=jnp.float32)
        multiscale_widths = jnp.array([0.01, 0.02, 0.05, 0.1], dtype=jnp.float32)
        scale_weights = jnp.ones((4,), dtype=jnp.float32)
        return {'byte_sequence': byte_sequence, 'continuous_positions': continuous_positions, 'emb': emb, 'locality_shapes': locality_shapes, 'w1': w1, 'b1': b1, 'w2': w2, 'b2': b2, 'w3': w3, 'b3': b3, 'multiscale_widths': multiscale_widths, 'scale_weights': scale_weights}
    _L0_tok_all = _L0_tok_setup()
    _L0_tok_in = {k: v for k, v in _L0_tok_all.items() if k in ('emb', 'locality_shapes', 'w1', 'b1', 'w2', 'b2', 'w3', 'b3', 'multiscale_widths', 'scale_weights')}
    del _L0_tok_all

    def _L0_attn_setup():
        import jax, jax.numpy as jnp
        import numpy as np
        import math
        key = jax.random.key(seed)
        ks = jax.random.split(key, 7)
        d_input, d_state, d_output = (64, 64, 64)
        B_, S_ = (8, 1024)
        x = jax.random.normal(ks[0], (B_, S_, d_input), dtype=jnp.float32)
        log_lambda_real = jax.random.normal(ks[1], (d_state,), dtype=jnp.float32)
        lambda_imag = jax.random.normal(ks[2], (d_state,), dtype=jnp.float32)
        dt = jnp.clip(0.01 + jax.random.normal(ks[3], (d_state,), dtype=jnp.float32) * 0.01, 0.005, 0.1)
        log_dt = jnp.log(dt)
        B = jax.random.normal(ks[4], (d_state, d_input), dtype=jnp.float32) / d_state ** 0.5
        C_real = jax.random.normal(ks[5], (d_output, d_state), dtype=jnp.float32) / d_state ** 0.5
        C_imag = jax.random.normal(ks[6], (d_output, d_state), dtype=jnp.float32) / d_state ** 0.5
        return {'x': x, 'log_lambda_real': log_lambda_real, 'lambda_imag': lambda_imag, 'log_dt': log_dt, 'B': B, 'C_real': C_real, 'C_imag': C_imag}
    _L0_attn_all = _L0_attn_setup()
    _L0_attn_in = {k: v for k, v in _L0_attn_all.items() if k in ('log_lambda_real', 'lambda_imag', 'log_dt', 'B', 'C_real', 'C_imag')}
    del _L0_attn_all

    def _L0_ffn_setup():
        import jax, jax.numpy as jnp
        import numpy as np
        C = 64
        HID = 256
        E = 8
        TEMP = 1.0
        key = jax.random.key(seed)
        ks = jax.random.split(key, 7)
        x = jax.random.normal(ks[0], (8, 4096, C), dtype=jnp.float32)
        W1 = jax.random.normal(ks[1], (C, HID), dtype=jnp.float32) * 0.02
        b1 = jnp.zeros((HID,), dtype=jnp.float32)
        Wg = jax.random.normal(ks[2], (HID, E), dtype=jnp.float32) * 0.02
        bg = jnp.zeros((E,), dtype=jnp.float32)
        Wd = jax.random.normal(ks[3], (E, HID, C), dtype=jnp.float32) * 0.02
        bd = jnp.zeros((E, C), dtype=jnp.float32)
        return {'x': x, 'W1': W1, 'b1': b1, 'Wg': Wg, 'bg': bg, 'Wd': Wd, 'bd': bd}
    _L0_ffn_all = _L0_ffn_setup()
    _L0_ffn_in = {k: v for k, v in _L0_ffn_all.items() if k in ('W1', 'b1', 'Wg', 'bg', 'Wd', 'bd')}
    del _L0_ffn_all
    return {'x': x, 'fside_BS_continuous_positions': fside_BS_continuous_positions, 'L0_tok_emb': _L0_tok_in['emb'], 'L0_tok_locality_shapes': _L0_tok_in['locality_shapes'], 'L0_tok_w1': _L0_tok_in['w1'], 'L0_tok_b1': _L0_tok_in['b1'], 'L0_tok_w2': _L0_tok_in['w2'], 'L0_tok_b2': _L0_tok_in['b2'], 'L0_tok_w3': _L0_tok_in['w3'], 'L0_tok_b3': _L0_tok_in['b3'], 'L0_tok_multiscale_widths': _L0_tok_in['multiscale_widths'], 'L0_tok_scale_weights': _L0_tok_in['scale_weights'], 'L0_attn_log_lambda_real': _L0_attn_in['log_lambda_real'], 'L0_attn_lambda_imag': _L0_attn_in['lambda_imag'], 'L0_attn_log_dt': _L0_attn_in['log_dt'], 'L0_attn_B': _L0_attn_in['B'], 'L0_attn_C_real': _L0_attn_in['C_real'], 'L0_attn_C_imag': _L0_attn_in['C_imag'], 'L0_ffn_W1': _L0_ffn_in['W1'], 'L0_ffn_b1': _L0_ffn_in['b1'], 'L0_ffn_Wg': _L0_ffn_in['Wg'], 'L0_ffn_bg': _L0_ffn_in['bg'], 'L0_ffn_Wd': _L0_ffn_in['Wd'], 'L0_ffn_bd': _L0_ffn_in['bd']}

def reference(x, fside_BS_continuous_positions, L0_tok_emb, L0_tok_locality_shapes, L0_tok_w1, L0_tok_b1, L0_tok_w2, L0_tok_b2, L0_tok_w3, L0_tok_b3, L0_tok_multiscale_widths, L0_tok_scale_weights, L0_attn_log_lambda_real, L0_attn_lambda_imag, L0_attn_log_dt, L0_attn_B, L0_attn_C_real, L0_attn_C_imag, L0_ffn_W1, L0_ffn_b1, L0_ffn_Wg, L0_ffn_bg, L0_ffn_Wd, L0_ffn_bd):
    import jax
    import jax.numpy as jnp

    def _L0_tok_ref(byte_sequence, continuous_positions, emb, locality_shapes, w1, b1, w2, b2, w3, b3, multiscale_widths, scale_weights):
        import jax, jax.numpy as jnp
        import numpy as np
        N_SCALES = 4

        def _conv1d(x, w, b, pad):
            y = jax.lax.conv_general_dilated(x, w, window_strides=(1,), padding=[(pad, pad)], dimension_numbers=('NCH', 'OIH', 'NCH'))
            return y + b[None, :, None]
        B, S = byte_sequence.shape
        P = continuous_positions.shape[1]
        amps = emb[byte_sequence]
        onehot = jax.nn.one_hot(byte_sequence, 64, dtype=jnp.float32)
        onehot = jnp.transpose(onehot, (0, 2, 1))
        h = jax.nn.gelu(_conv1d(onehot, w1, b1, 3), approximate=False)
        h = jax.nn.gelu(_conv1d(h, w2, b2, 2), approximate=False)
        ctx = jax.nn.sigmoid(_conv1d(h, w3, b3, 1))[:, 0, :]
        amps = amps * ctx[:, :, None]
        lp = locality_shapes[byte_sequence]
        byte_pos = jnp.linspace(0.0, 1.0, S, dtype=jnp.float32)
        center = byte_pos[None, :] + lp[..., 0] * 0.05
        xd = continuous_positions[:, None, :] - center[..., None]
        amp_scale = jax.nn.sigmoid(lp[..., 2])
        phase = lp[..., 3] * jnp.pi
        abs_w = jnp.abs(lp[..., 1])
        TWO_PI = 2.0 * jnp.pi
        basis_total = jnp.zeros((B, S, P), dtype=jnp.float32)
        for s in range(N_SCALES):
            width = abs_w * multiscale_widths[s] + 1e-05
            z = xd / width[..., None]
            basis = jnp.exp(-0.5 * z * z) * jnp.cos(phase[..., None] + TWO_PI * z)
            basis_total = basis_total + basis * (amp_scale[..., None] * scale_weights[s] ** 2)
        semantic_field = jnp.einsum('bsp,bsd->bpd', basis_total, amps)
        return semantic_field

    def _L0_attn_ref(x, log_lambda_real, lambda_imag, log_dt, B, C_real, C_imag):
        import jax, jax.numpy as jnp
        import numpy as np
        import math
        batch, seq_len, _ = x.shape
        Lambda = -jnp.exp(log_lambda_real) + 1j * lambda_imag
        dt = jnp.clip(jnp.exp(log_dt), 0.005, 0.1)
        denom = 1.0 - 0.5 * dt * Lambda
        A_bar = (1.0 + 0.5 * dt * Lambda) / denom
        B_bar = (dt / denom)[:, None] * B
        u = jnp.matmul(x, B_bar.real.T) + 1j * jnp.matmul(x, B_bar.imag.T)
        A_poles = jnp.broadcast_to(A_bar[:, None], (A_bar.shape[0], seq_len))
        A_cp = jnp.cumprod(A_poles, axis=1)
        A_powers = jnp.concatenate([jnp.ones_like(A_cp[:, :1]), A_cp[:, :-1]], axis=1)
        n_fft = 2 ** math.ceil(math.log2(seq_len * 2 - 1))
        u_t = jnp.swapaxes(u, 1, 2)
        u_f = jnp.fft.fft(u_t, n=n_fft, axis=-1)
        A_f = jnp.fft.fft(A_powers, n=n_fft, axis=-1)
        h = jnp.fft.ifft(u_f * A_f[None], n=n_fft, axis=-1)[..., :seq_len]
        h = jnp.swapaxes(h, 1, 2)
        C_c = C_real + 1j * C_imag
        return jnp.matmul(h, C_c.T).real

    def _L0_ffn_ref(x, W1, b1, Wg, bg, Wd, bd):
        import jax, jax.numpy as jnp
        import numpy as np
        C = 64
        HID = 256
        E = 8
        TEMP = 1.0
        orig_shape = x.shape
        xf = x.reshape(-1, orig_shape[-1])
        H = jax.nn.gelu(xf @ W1 + b1, approximate=False)
        probs = jax.nn.softmax((H @ Wg + bg) / TEMP, axis=-1)
        assign = jnp.argmax(probs, axis=-1)
        out = jnp.zeros_like(xf)
        for e in range(Wd.shape[0]):
            y = H @ Wd[e] + bd[e]
            sel = (assign == e)[:, None]
            out = out + jnp.where(sel, probs[:, e:e + 1] * y, 0.0)
        return out.reshape(orig_shape)
    h = _L0_tok_ref(x, fside_BS_continuous_positions, L0_tok_emb, L0_tok_locality_shapes, L0_tok_w1, L0_tok_b1, L0_tok_w2, L0_tok_b2, L0_tok_w3, L0_tok_b3, L0_tok_multiscale_widths, L0_tok_scale_weights)
    h = h + _L0_attn_ref(_layernorm(h, axis=-1), L0_attn_log_lambda_real, L0_attn_lambda_imag, L0_attn_log_dt, L0_attn_B, L0_attn_C_real, L0_attn_C_imag)
    h = h + _L0_ffn_ref(_layernorm(h, axis=-1), L0_ffn_W1, L0_ffn_b1, L0_ffn_Wg, L0_ffn_bg, L0_ffn_Wd, L0_ffn_bd)
    return h

_drawn_inputs = setup_inputs


def setup_inputs(seed=0):
    import zlib

    import numpy as np

    out = dict(_drawn_inputs(seed))
    spreads = {'L0_tok_b1': (0.0, 0.8),
     'L0_tok_b2': (0.0, 0.8),
     'L0_tok_scale_weights': (1.0, 0.2),
     'L0_ffn_b1': (0.0, 0.8),
     'L0_ffn_bg': (0.0, 0.533),
     'L0_ffn_bd': (0.0, 0.778)}
    factors = {'L0_tok_w1': 8.0,
     'L0_tok_w2': 8.0,
     'L0_tok_w3': 8.0,
     'L0_ffn_W1': 8.0,
     'L0_ffn_Wg': 8.0,
     'L0_ffn_Wd': 8.0}
    for name, (base, spread) in spreads.items():
        noise = np.random.default_rng([zlib.crc32(name.encode()), seed]).standard_normal(out[name].shape)
        drawn = base * np.exp(spread * noise) if base else spread * noise
        out[name] = jnp.asarray(drawn.astype(out[name].dtype))
    for name, factor in factors.items():
        out[name] = (out[name] * factor).astype(out[name].dtype)
    return out
```

```python
from contextlib import ExitStack

import concourse.bass as bass
import numpy as np
from concourse import mybir

ALU = mybir.AluOpType
ACT = mybir.ActivationFunctionType
F32 = mybir.dt.float32
BF16 = mybir.dt.bfloat16
I32 = mybir.dt.int32

P = 128
NB = 16
G = 4
GB = NB // G
T = GB * P
D = 64
V = 64
NL = 4
NS = 4
C1 = 128
K1, K2, K3 = 7, 5, 3
HID = 256
KH = HID // P
NE = 8
PADX = P + 6
PADH = P + 4
TURN = 2.0 ** 26
TURN_MASK = 0x3FFFFFC
PI_BELOW = 3.1415925
EPS = 1e-5
ROUND = 1.5 * 2.0 ** 23


STEPS = G + 4
FINISHED = (tuple(range(G - 2)), tuple(range(G - 2, G)))


def on(g):
    return 0 <= g < G


def columns(*parts):
    at, out = 0, {}
    for name, width in parts:
        out[name] = slice(at, at + width)
        at += width
    return out, at


SMALL, NSMALL = columns(
    ("shift", P + 2), ("half0", 1), ("half1", 1), ("value", 1), ("place", 1), ("emb", D + NL),
    ("b1", 1), ("b2", 1), ("b3", 1), ("widths", NS), ("weights", NS),
    ("log_re", 1), ("im", 1), ("log_dt", 1), ("w3", 2 * K3), ("ffn_b1", KH), ("bg", NE))
STATE, NSTATE = columns(("B", P), ("C_re", D), ("C_im", D), ("W1", HID), ("Wg", KH * NE))


def repeat(ap, axis, n):
    ap = ap.unsqueeze(axis)
    shape = list(ap.shape)
    shape[axis] = n
    return ap.broadcast_to(shape)


def tower(nc, x, positions, small, w1, w2, state, wd, bd, out):
    ctx = ExitStack()
    with ctx:
        def sb(name, shape, dt=F32):
            return ctx.enter_context(nc.sbuf_tensor(name, shape, dt))

        def sem(name):
            return ctx.enter_context(nc.semaphore(name))

        pair = [ctx.enter_context(nc.psum_tensor(f"pair{i}", [P, 2, T], F32)) for i in range(2)]
        bank = [pair[i // 2][:, i % 2, :] for i in range(4)]
        bank += [ctx.enter_context(nc.psum_tensor(f"bank{i}", [P, T], F32))[:, :] for i in range(4, 6)]
        chain_bank, logit_bank = bank[4], bank[5]
        hid_pair = ctx.enter_context(nc.psum_tensor("hid_pair", [P, 2, T], F32))
        bank += [hid_pair[:, i, :] for i in range(2)]

        sm = sb("sm", [P, NSMALL])
        w1_sb = sb("w1_sb", [P, 4, C1])
        w2_sb = sb("w2_sb", [P, K2, D])
        st_sb = sb("st_sb", [P, NSTATE])
        wd_sb = sb("wd_sb", [P, KH, NE * D])
        bd_sb = sb("bd_sb", [96, NE * D])
        posb = sb("posb", [P, NB, P])
        bytes_pad = sb("bytes_pad", [P, NB, PADX], I32)

        def col(name):
            return sm[:, SMALL[name]]

        identity = sm[:, SMALL["shift"].start + 1:SMALL["shift"].start + 1 + P]

        def shift(k):
            return sm[:, SMALL["shift"].start + k:SMALL["shift"].start + k + P]

        B_dup = st_sb[:, STATE["B"]]
        C_re = st_sb[:, STATE["C_re"]]
        W1 = st_sb[:, STATE["W1"]]
        Wg = st_sb[:, STATE["Wg"]].rearrange("p (k e) -> p k e", k=KH)

        onehot = sb("onehot", [P, NB, PADX], BF16)
        embp = [sb(f"embp{i}", [V, D + NL], BF16) for i in range(3)]
        embr = [sb(f"embr{i}", [V, D + NL]) for i in range(2)]
        w1p = [sb(f"w1p{i}", [P, 4, C1], BF16) for i in range(3)]
        w1r = [sb(f"w1r{i}", [P, 4, C1]) for i in range(2)]
        bdp = sb("bdp", [96, NE * D], BF16)
        bdh = [sb(f"bdh{i}", [96, NE * D], BF16) for i in range(2)]
        bdr = [sb(f"bdr{i}", [96, NE * D]) for i in range(2)]
        ones = sb("ones", [96, P], BF16)
        tok = sb("tok", [P, NB, D + NL])
        h1 = sb("h1", [P, NB, PADH])
        h2 = sb("h2", [P, G // 2, GB, P])
        taps = sb("taps", [P, NB, K3])
        neg_b3 = sb("neg_b3", [P, 1])
        ctx_exp = sb("ctx_exp", [P, NB])
        amp_exp = sb("amp_exp", [P, NB])
        amp_tmp = sb("amp_tmp", [P, 3, NB])
        gain = sb("gain", [P, NB])
        amps = sb("amps", [P, NB, D])
        center = sb("center", [P, NB])
        absw = sb("absw", [P, NB])
        inv_width = sb("inv_width", [P, G, NS, GB])
        width = sb("width", [P, G, NS, GB])
        phase_tmp = sb("phase_tmp", [P, 3, NB])
        phase = sb("phase", [P, G, NS, GB])
        scale_w = sb("scale_w", [P, NS])
        dist = sb("dist", [P, NB, P])
        picked = posb[:, 0:8, :].rearrange("p b t -> p (b t)").rearrange("p (g b d) -> p g b d", g=G, b=GB)
        wave = sb("wave", [P, G, NS * T])
        angle = sb("angle", [P, G, NS * T], I32)
        bell = sb("bell", [P, G, NS * T])
        basis = sb("basis", [P, G, T])
        neg_pi = sb("neg_pi", [P, 1])
        minus_half = sb("minus_half", [P, NB])
        zero_one = sb("zero_one", [P, 1])

        h_a = sb("h_a", [P, G, GB, D])
        h_b = sb("h_b", [P, G, GB, D])
        stats = sb("stats", [P, 2, G, GB, 6])
        mean_var = sb("mean_var", [P, 2, G, GB, 2])
        var_eps = sb("var_eps", [P, 2, G, GB])
        rstd = sb("rstd", [P, 2, G, GB])
        turned = wave[:, :, 0:2 * T].rearrange("p g (r t) -> p g r t", r=2)
        drive = wave[:, :, 2 * T:3 * T]
        modes = wave[:, :, 3 * T:4 * T]
        spent = angle[:, :, :].bitcast(F32)
        W = GB * D

        def spent_rows(k):
            return spent[:, :, k * W:(k + 1) * W].rearrange("p g (b d) -> p g b d", b=GB)

        cent, normed = [spent_rows(0), spent_rows(1)], [spent_rows(2), spent_rows(3)]
        xT, x2T = (spent[:, :, k * W:(k + 1) * W].rearrange("p g (b t) -> p g b t", b=2) for k in (4, 5))
        scaled, result = spent_rows(6), spent_rows(7)
        H = bell[:, :, 0:KH * T].rearrange("p g (k t) -> p g k t", k=KH)
        neg_C_im = sb("neg_C_im", [P, D])
        spar = sb("spar", [P, 32])
        powers = sb("powers", [P, 2, P + 1])
        ptmp = sb("ptmp", [P, 4, P])
        drive_tab = sb("drive_tab", [P, P])
        turn_tab = sb("turn_tab", [P, 2, P])
        decay = sb("decay", [P, GB, P])
        logits = sb("logits", [P, G, GB, NE])
        top = sb("top", [P, G, GB])
        below = sb("below", [P, G, GB, NE])
        chosen = sb("chosen", [P, G, GB, NE], I32)
        expl = sb("expl", [P, G, GB, NE])
        denom = sb("denom", [P, G, GB])
        prob = sb("prob", [P, G, GB])

        ld = {n: sem(f"ld_{n}") for n in ("x", "pos", "small", "w1", "w2", "state", "wd", "bd")}
        stored = sem("stored")
        dve_chain, pool_chain = sem("dve_chain"), sem("pool_chain")
        s_pad = sem("s_pad")
        s_cst = sem("s_cst")
        s_emb_split = sem("s_emb_split")
        s_onehot = sem("s_onehot")
        s_w1_split = sem("s_w1_split")
        s_bd_split = sem("s_bd_split")
        s_emb_mm, s_tok = sem("s_emb_mm"), sem("s_tok")
        s_conv1, s_h1 = sem("s_conv1"), sem("s_h1")
        s_conv2, s_h2 = sem("s_conv2"), sem("s_h2")
        s_taps_mm, s_taps = sem("s_taps_mm"), sem("s_taps")
        s_ctx_mm, s_ctx = sem("s_ctx_mm"), sem("s_ctx")
        s_amp_exp, s_negb3 = sem("s_amp_exp"), sem("s_negb3")
        s_gain, s_amps = sem("s_gain"), sem("s_amps")
        s_z, s_angle = sem("s_z"), sem("s_angle")
        s_square, s_bell, s_cos = sem("s_square"), sem("s_bell"), sem("s_cos")
        s_prod, s_basis = sem("s_prod"), sem("s_basis")
        s_sexp, s_spar_neg = sem("s_sexp"), sem("s_spar_neg")
        s_tables = sem("s_tables")
        s_field, s_ha = sem("s_field"), sem("s_ha")
        s_mv = [sem("s_mv0"), sem("s_mv1")]
        s_rstd = [sem("s_rstd0"), sem("s_rstd1")]
        s_normed = [sem("s_normed0"), sem("s_normed1")]
        s_turn = [sem("s_turn0"), sem("s_turn1")]
        s_xT = [sem("s_xT0"), sem("s_xT1")]
        s_v, s_drive = sem("s_v"), sem("s_drive")
        s_turned = sem("s_turned")
        s_y, s_hb = sem("s_y"), sem("s_hb")
        s_hid, s_H = sem("s_hid"), sem("s_H")
        s_logit, s_lread, s_below = sem("s_logit"), sem("s_lread"), sem("s_below")
        s_expl, s_prob = sem("s_expl"), sem("s_prob")
        s_exp_mm, s_pick = sem("s_exp_mm"), sem("s_pick")
        s_result = sem("s_result")

        block = ctx.enter_context(nc.Block())

        @block.sync
        def _(sp):
            sp.dma_start(sm[:, :], small).then_inc(ld["small"], 16)
            sp.wait_ge(s_pad, 1)
            for half in range(2):
                rows = slice(half * V, half * V + V)
                sp.dma_start(bytes_pad[rows, :, 3 - half:3 - half + P],
                             repeat(x, 0, V)).then_inc(ld["x"], 16)
            sp.dma_start(w1_sb[:, :, :], w1).then_inc(ld["w1"], 16)
            sp.dma_start(posb[:, :, :],
                         repeat(positions, 0, P)).then_inc(ld["pos"], 16)
            sp.dma_start(w2_sb[:, :, :], w2).then_inc(ld["w2"], 16)
            sp.dma_start(st_sb[:, :], state).then_inc(ld["state"], 16)
            sp.dma_start(bd_sb[:, :], bd).then_inc(ld["bd"], 16)
            sp.dma_start(wd_sb[:, :, :], wd).then_inc(ld["wd"], 16)
            for g in range(G):
                sp.wait_ge(s_result, g + 1)
                sp.dma_start(out[g * GB:(g + 1) * GB].rearrange("b p d -> p b d"),
                             result[:, g]).then_inc(stored, 16)
            sp.wait_ge(stored, 16 * G)

        @block.gpsimd
        def _(pool):
            count = [0]

            def link(ins):
                count[0] += 1
                ins.then_inc(pool_chain, 1)
                pool.wait_ge(pool_chain, count[0])

            pool.memset(bytes_pad[:, :, :], -1).then_inc(s_pad, 1)
            pool.memset(neg_pi[:, :], -PI_BELOW)
            pool.memset(h1[:, :, 0:2], 0.0)
            pool.memset(h1[:, :, 2 + P:], 0.0)
            pool.memset(ones[:, :], 1.0).then_inc(s_cst, 1)

            pool.wait_ge(ld["w1"], 16)
            link(pool.tensor_copy(w1p[0][:], w1_sb[:]))
            link(pool.tensor_tensor(w1r[0][:], w1_sb[:], w1p[0][:], ALU.subtract))
            link(pool.tensor_copy(w1p[1][:], w1r[0][:]))
            link(pool.tensor_tensor(w1r[1][:], w1r[0][:], w1p[1][:], ALU.subtract))
            pool.tensor_copy(w1p[2][:], w1r[1][:]).then_inc(s_w1_split, 1)

            link(pool.memset(minus_half[:, :], -0.5))
            slot = iter(range(32))

            def new():
                k = next(slot)
                return spar[:, k:k + 1]

            lam, dt = new(), new()

            pool.wait_ge(s_sexp, 2)
            dtc, hr, hi = new(), new(), new()
            link(pool.tensor_scalar(dtc, dt, 0.005, 0.1, ALU.max, ALU.min))
            link(pool.tensor_tensor(hr, dtc, lam, ALU.mult))
            link(pool.tensor_scalar(hr, hr, -0.5, None, ALU.mult))
            link(pool.tensor_tensor(hi, dtc, col("im"), ALU.mult))
            link(pool.tensor_scalar(hi, hi, 0.5, None, ALU.mult))
            low, high, hi2, d2, n2, inv = new(), new(), new(), new(), new(), new()
            link(pool.tensor_scalar(low, hr, -1.0, 1.0, ALU.mult, ALU.add))
            link(pool.tensor_scalar(high, hr, 1.0, None, ALU.add))
            link(pool.tensor_tensor(hi2, hi, hi, ALU.mult))
            link(pool.tensor_tensor(d2, low, low, ALU.mult))
            link(pool.tensor_tensor(d2, d2, hi2, ALU.add))
            link(pool.tensor_tensor(n2, high, high, ALU.mult))
            link(pool.tensor_tensor(n2, n2, hi2, ALU.add))
            link(pool.tensor_tensor(inv, d2, minus_half[:, 0:1], ALU.pow))
            link(pool.tensor_tensor(inv, inv, inv, ALU.mult))
            rho2, rho, irho, zero = new(), new(), new(), new()
            link(pool.tensor_tensor(rho2, n2, inv, ALU.mult))
            link(pool.tensor_scalar(zero, rho2, 1e-30, None, ALU.is_lt))
            link(pool.tensor_scalar(rho, rho2, 1e-30, None, ALU.max))
            link(pool.tensor_tensor(irho, rho, minus_half[:, 0:1], ALU.pow))
            link(pool.tensor_tensor(rho, rho2, irho, ALU.mult))
            link(pool.tensor_tensor(irho, irho, inv, ALU.mult))
            keep, c1, s1 = new(), new(), new()
            link(pool.tensor_scalar(keep, zero, -1.0, 1.0, ALU.mult, ALU.add))
            link(pool.tensor_tensor(irho, irho, keep, ALU.mult))
            link(pool.tensor_tensor(c1, low, high, ALU.mult))
            link(pool.tensor_tensor(c1, c1, hi2, ALU.subtract))
            link(pool.tensor_tensor(c1, c1, irho, ALU.mult))
            link(pool.tensor_tensor(powers[:, 0, 1:2], c1, zero, ALU.add))
            link(pool.tensor_scalar(s1, hi, 2.0, None, ALU.mult))
            link(pool.tensor_tensor(powers[:, 1, 1:2], s1, irho, ALU.mult))
            link(pool.memset(powers[:, 0, 0:1], 1.0))
            link(pool.memset(powers[:, 1, 0:1], 0.0))
            m = 1
            while m < P:
                c, s = powers[:, 0, m:m + 1], powers[:, 1, m:m + 1]
                link(pool.tensor_scalar(ptmp[:, 0:2, 0:m], powers[:, :, 1:m + 1], c, None, ALU.mult))
                link(pool.tensor_scalar(ptmp[:, 2:4, 0:m], powers[:, :, 1:m + 1], s, None, ALU.mult))
                link(pool.tensor_tensor(powers[:, 0, m + 1:2 * m + 1], ptmp[:, 0, 0:m], ptmp[:, 3, 0:m],
                                        ALU.subtract))
                link(pool.tensor_tensor(powers[:, 1, m + 1:2 * m + 1], ptmp[:, 1, 0:m], ptmp[:, 2, 0:m],
                                        ALU.add))
                m *= 2
            b_re, b_im, mix_c, mix_s, t0 = new(), new(), new(), new(), new()
            link(pool.tensor_tensor(t0, dtc, inv, ALU.mult))
            link(pool.tensor_tensor(b_re, t0, low, ALU.mult))
            link(pool.tensor_tensor(b_im, t0, hi, ALU.mult))
            link(pool.tensor_tensor(mix_c, b_re, col("half0"), ALU.mult))
            link(pool.tensor_tensor(t0, b_im, col("half1"), ALU.mult))
            link(pool.tensor_tensor(mix_c, mix_c, t0, ALU.add))
            link(pool.tensor_tensor(mix_s, b_im, col("half0"), ALU.mult))
            link(pool.tensor_tensor(t0, b_re, col("half1"), ALU.mult))
            link(pool.tensor_tensor(mix_s, mix_s, t0, ALU.subtract))
            cos_t, sin_t = powers[:, 0, 0:P], powers[:, 1, 0:P]
            link(pool.tensor_scalar(ptmp[:, 0, :], cos_t, mix_c, None, ALU.mult))
            link(pool.tensor_scalar(ptmp[:, 1, :], sin_t, mix_s, None, ALU.mult))
            link(pool.tensor_tensor(drive_tab[:, :], ptmp[:, 0, :], ptmp[:, 1, :], ALU.add))
            link(pool.tensor_scalar(ptmp[:, 0, :], cos_t, col("half0"), None, ALU.mult))
            link(pool.tensor_scalar(ptmp[:, 1, :], sin_t, col("half1"), None, ALU.mult))
            link(pool.tensor_tensor(turn_tab[:, 0, :], ptmp[:, 0, :], ptmp[:, 1, :], ALU.subtract))
            link(pool.tensor_scalar(ptmp[:, 2, :], sin_t, col("half0"), None, ALU.mult))
            link(pool.tensor_scalar(ptmp[:, 3, :], cos_t, col("half1"), None, ALU.mult))
            link(pool.tensor_tensor(turn_tab[:, 1, :], ptmp[:, 2, :], ptmp[:, 3, :], ALU.add))
            link(pool.memset(decay[:, :, :], 1.0))
            link(pool.tensor_scalar(decay[:, :, :], decay[:, :, :], rho, None, ALU.mult))
            link(pool.memset(decay[:, :, 0:1], 0.0))
            pool.wait_ge(ld["state"], 16)
            pool.tensor_scalar(neg_C_im[:, :], st_sb[:, STATE["C_im"]], -1.0, None, ALU.mult).then_inc(s_tables, 1)

            pool.wait_ge(ld["bd"], 16)
            link(pool.tensor_copy(bdh[0][:], bd_sb[:]))
            link(pool.tensor_tensor(bdr[0][:], bd_sb[:], bdh[0][:], ALU.subtract))
            link(pool.tensor_copy(bdh[1][:], bdr[0][:]))
            link(pool.tensor_tensor(bdr[1][:], bdr[0][:], bdh[1][:], ALU.subtract))
            link(pool.tensor_copy(bdp[0:32, :], bdh[0][0:32, :]))
            link(pool.tensor_copy(bdp[32:64, :], bdh[1][32:64, :]))
            link(pool.tensor_copy(bdp[64:96, :], bdr[1][64:96, :]))
            pool.wait_ge(s_z, 1)
            pool.memset(picked[:, :, :, :], 0.0).then_inc(s_bd_split, 1)

            for g in range(G):
                b = slice(g * GB, (g + 1) * GB)
                pool.wait_ge(s_gain, 1)
                pool.tensor_tensor(amps[:, b, :], tok[:, b, 0:D],
                                   repeat(gain[:, b], 2, D), ALU.mult).then_inc(s_amps, 1)

            def sum_scales(g):
                pool.wait_ge(s_prod, NS * (g + 1))
                w = bell[:, g, :].rearrange("p (s t) -> p s t", s=NS)
                link(pool.tensor_tensor(w[:, 0:2, :], w[:, 0:2, :], w[:, 2:4, :], ALU.add))
                pool.tensor_tensor(basis[:, g, :], w[:, 0, :], w[:, 1, :], ALU.add).then_inc(s_basis, 1)

            def inv_std(n, g):
                pool.wait_ge(s_mv[n], g + 1)
                link(pool.tensor_scalar(var_eps[:, n, g, :], mean_var[:, n, g, :, 1], EPS, None, ALU.add))
                pool.tensor_tensor(rstd[:, n, g, :], var_eps[:, n, g, :], minus_half[:, 0:GB],
                                   ALU.pow).then_inc(s_rstd[n], 1)

            def finish(g):
                if g == 0:
                    pool.wait_ge(s_prob, 1)
                pool.wait_ge(s_pick, 2 * (g + 1))
                link(pool.tensor_tensor(
                    scaled[:, g].rearrange("p (b h) d -> p b h d", h=2),
                    picked[:, g].rearrange("p (b h) d -> p b h d", h=2),
                    repeat(prob[:, g].rearrange("p (h b) -> p b h", h=2), 3, D), ALU.mult))
                pool.tensor_tensor(result[:, g], scaled[:, g], h_b[:, g], ALU.add).then_inc(s_result, 1)

            for i in range(STEPS):
                if on(i - 1):
                    inv_std(0, i - 1)
                if on(i - 2):
                    inv_std(1, i - 2)
                if on(i):
                    sum_scales(i)
                if i >= G + 2:
                    for g in FINISHED[i - G - 2]:
                        finish(g)

        @block.scalar
        def _(act):
            act.wait_ge(ld["small"], 16)
            act.activation(spar[:, 0:1], col("log_re"), ACT.Exp).then_inc(s_sexp, 1)
            act.activation(spar[:, 1:2], col("log_dt"), ACT.Exp).then_inc(s_sexp, 1)
            act.activation(neg_b3[:, :], col("b3"), ACT.Copy, scale=-1.0).then_inc(s_negb3, 1)
            for g in range(G):
                act.wait_ge(s_emb_mm, g + 1)
                act.copy(tok[:, g * GB:(g + 1) * GB, :],
                         bank[4 + g][:, 0:GB * (D + NL)].rearrange("p (b c) -> p b c", b=GB)).then_inc(s_tok, 1)
            act.wait_ge(s_tok, G)
            act.activation(amp_exp[:, :], tok[:, :, D + 2], ACT.Exp, scale=-1.0).then_inc(s_amp_exp, 1)
            act.wait_ge(s_cst, 1)
            for g in range(G):
                act.wait_ge(s_conv1, g + 1)
                act.activation(h1[:, g * GB:(g + 1) * GB, 2:2 + P],
                               bank[g].rearrange("p (b s) -> p b s", b=GB), ACT.Gelu,
                               bias=col("b1")).then_inc(s_h1, 1)
            for g in range(G):
                act.wait_ge(s_z, g + 1)
                act.activation(bell[:, g, :], wave[:, g, :], ACT.Square).then_inc(s_square, 1)
                act.wait_ge(s_square, g + 1)
                act.activation(bell[:, g, :], bell[:, g, :], ACT.Exp, scale=-0.5).then_inc(s_bell, 1)
            for q in range(G // 2):
                act.wait_ge(s_conv2, q + 1)
                act.activation(h2[:, q, :, :].rearrange("p b s -> p (b s)"), bank[2 * q], ACT.Gelu,
                               bias=col("b2")).then_inc(s_h2, 1)
            act.wait_ge(s_ctx_mm, 1)
            act.wait_ge(s_negb3, 1)
            act.activation(ctx_exp[:, :], bank[3][:, 0:NB], ACT.Exp, bias=neg_b3[:, 0:1],
                           scale=-1.0).then_inc(s_ctx, 1)

            def cosine(g):
                act.wait_ge(s_angle, g + 1)
                act.wait_ge(s_bell, g + 1)
                act.activation(wave[:, g, :], angle[:, g, :], ACT.Sin, bias=neg_pi[:, 0:1],
                               scale=2.0 * PI_BELOW / TURN).then_inc(s_cos, 1)

            def field_out(g):
                act.wait_ge(s_field, g + 1)
                act.copy(h_a[:, g, :, :].rearrange("p b d -> p (b d)"), bank[g][:, 0:GB * D]).then_inc(s_ha, 1)

            def transposed_out(n, g):
                act.wait_ge(s_turn[n], g + 1)
                src = (chain_bank, bank[6])[n]
                act.copy((xT, x2T)[n][:, g].rearrange("p b t -> p (b t)"), src[:, 0:2 * P]).then_inc(s_xT[n], 1)

            def hidden(g):
                act.wait_ge(s_hid, g + 1)
                for k in range(KH):
                    act.activation(H[:, g, k, :].rearrange("p (h t) -> p h t", h=2),
                                   hid_pair[:, :, k * 2 * P:(k + 1) * 2 * P], ACT.Gelu,
                                   bias=sm[:, SMALL["ffn_b1"].start + k:SMALL["ffn_b1"].start + k + 1]).then_inc(s_H, 1)

            cosine(0)
            cosine(1)
            for i in range(STEPS - 2):
                if on(i - 1):
                    transposed_out(0, i - 1)
                if on(i - 2):
                    transposed_out(1, i - 2)
                    hidden(i - 2)
                if on(i):
                    field_out(i)
                if on(i + 2):
                    cosine(i + 2)
            act.wait_ge(s_below, G)
            act.activation(expl[:, :, :, :], below[:, :, :, :], ACT.Exp).then_inc(s_expl, 1)

        @block.vector
        def _(dve):
            count = [0]

            def link(ins):
                count[0] += 1
                ins.then_inc(dve_chain, 1)
                dve.wait_ge(dve_chain, count[0])

            dve.wait_ge(ld["small"], 16)
            table = sm[0:V, SMALL["emb"]]
            link(dve.tensor_copy(embp[0][:], table))
            link(dve.tensor_tensor(embr[0][:], table, embp[0][:], ALU.subtract))
            link(dve.tensor_copy(embp[1][:], embr[0][:]))
            link(dve.tensor_tensor(embr[1][:], embr[0][:], embp[1][:], ALU.subtract))
            dve.tensor_copy(embp[2][:], embr[1][:]).then_inc(s_emb_split, 1)
            link(dve.tensor_tensor(scale_w[:, :], col("weights"), col("weights"), ALU.mult))
            dve.wait_ge(ld["x"], 32)
            dve.tensor_scalar(onehot[:, :, :], bytes_pad[:, :, :], col("value"), None,
                              ALU.is_equal).then_inc(s_onehot, 1)

            dve.wait_ge(s_tok, G)
            lp = [tok[:, :, D + k] for k in range(NL)]
            dve.tensor_scalar(center[:, :], lp[0], 0.05, col("place"), ALU.mult, ALU.add)
            link(dve.scalar_tensor_tensor(out=absw[:, :], in0=lp[1], scalar=-1.0, in1=lp[1], op0=ALU.mult, op1=ALU.max))
            for s in range(NS):
                c = SMALL["widths"].start + s
                ins = dve.tensor_scalar(width[:, :, s, :], absw[:, :].rearrange("p (g b) -> p g b", g=G),
                                        sm[:, c:c + 1], 1e-5, ALU.mult, ALU.add)
            link(ins)
            link(dve.reciprocal(inv_width[:, :, :, :], width[:, :, :, :]))
            dve.wait_ge(ld["pos"], 16)
            link(dve.tensor_tensor(dist[:, :, :], posb[:, :, :], repeat(center[:, :], 2, P),
                                   ALU.subtract))
            for g in range(G):
                zs = wave[:, g, :].rearrange("p (s b t) -> p s b t", s=NS, b=GB)
                dve.tensor_tensor(
                    wave[:, g, :].rearrange("p (s t) -> p s t", s=NS),
                    repeat(dist[:, g * GB:(g + 1) * GB, :].rearrange("p b t -> p (b t)"), 1, NS),
                    repeat(inv_width[:, g, :, :].rearrange("p s b -> p (s b)"), 2, P),
                    ALU.mult).then_inc(s_z, 1)
            link(dve.tensor_scalar(phase_tmp[:, 0, :], lp[3], 0.5, ROUND, ALU.mult, ALU.add))
            link(dve.tensor_scalar(phase_tmp[:, 1, :], phase_tmp[:, 0, :], -ROUND, None, ALU.add))
            link(dve.scalar_tensor_tensor(out=phase_tmp[:, 2, :], in0=lp[3], scalar=0.5, in1=phase_tmp[:, 1, :],
                                          op0=ALU.mult, op1=ALU.subtract))
            link(dve.tensor_scalar(phase[:, :, :, :],
                                   repeat(phase_tmp[:, 2, :].rearrange("p (g b) -> p g b", g=G), 2, NS),
                                   0.75, TURN, ALU.add, ALU.mult))
            for g in range(G):
                dve.wait_ge(s_z, g + 1)
                link(dve.scalar_tensor_tensor(
                    out=angle[:, g, :].rearrange("p (s t) -> p s t", t=P),
                    in0=wave[:, g, :].rearrange("p (s t) -> p s t", t=P), scalar=TURN,
                    in1=repeat(phase[:, g, :, :].rearrange("p s b -> p (s b)"), 2, P),
                    op0=ALU.mult, op1=ALU.add))
                dve.tensor_scalar(angle[:, g, :], angle[:, g, :], TURN_MASK, None,
                                  ALU.bitwise_and).then_inc(s_angle, 1)

            dve.wait_ge(s_taps_mm, 1)
            dve.tensor_copy(taps[:, :, :].rearrange("p b k -> p (b k)"), bank[1][:, 0:NB * K3]).then_inc(s_taps, 1)
            dve.wait_ge(s_amp_exp, 1)
            link(dve.tensor_scalar(amp_tmp[:, 0, :], amp_exp[:, :], 1.0, None, ALU.add))
            dve.wait_ge(s_ctx, 1)
            link(dve.scalar_tensor_tensor(
                out=amp_tmp[:, 1, :].rearrange("p (q r b) -> p q r b", q=2, r=2)[:, 0],
                in0=ctx_exp[:, 0:8].rearrange("p (b r) -> p r b", r=2), scalar=1.0,
                in1=amp_tmp[:, 0, 0:8].rearrange("p (r b) -> p r b", r=2), op0=ALU.add, op1=ALU.mult))
            link(dve.scalar_tensor_tensor(
                out=amp_tmp[:, 1, :].rearrange("p (q r b) -> p q r b", q=2, r=2)[:, 1],
                in0=ctx_exp[:, 8:16].rearrange("p (b r) -> p r b", r=2), scalar=1.0,
                in1=amp_tmp[:, 0, 8:16].rearrange("p (r b) -> p r b", r=2), op0=ALU.add, op1=ALU.mult))
            dve.reciprocal(gain[:, :], amp_tmp[:, 1, :]).then_inc(s_gain, 1)

            def product(g):
                dve.wait_ge(s_cos, g + 1)
                for s in range(NS):
                    part = slice(s * T, (s + 1) * T)
                    dve.scalar_tensor_tensor(out=bell[:, g, part], in0=bell[:, g, part],
                                             scalar=scale_w[:, s:s + 1], in1=wave[:, g, part],
                                             op0=ALU.mult, op1=ALU.mult).then_inc(s_prod, 1)

            def norm(n, g, src):
                for b in range(GB):
                    ins = dve.bn_stats(stats[:, n, g, b, :], src[:, g, b, :])
                link(ins)
                for b in range(GB):
                    ins = dve.bn_aggr(mean_var[:, n, g, b, :], stats[:, n, g, b, :])
                ins.then_inc(s_mv[n], 1)
                dve.wait_ge(s_mv[n], g + 1)
                link(dve.tensor_tensor(cent[n][:, g], src[:, g, :, :],
                                       repeat(mean_var[:, n, g, :, 0], 2, D), ALU.subtract))
                dve.wait_ge(s_rstd[n], g + 1)
                dve.tensor_tensor(normed[n][:, g], cent[n][:, g],
                                  repeat(rstd[:, n, g, :], 2, D), ALU.mult).then_inc(s_normed[n], 1)

            def norm_a(g):
                dve.wait_ge(s_ha, g + 1)
                norm(0, g, h_a)

            def recurrence(g):
                if g == 0:
                    dve.wait_ge(s_tables, 1)
                dve.wait_ge(s_v, 2 * (g + 1))
                dve.tensor_tensor(drive[:, g, :].rearrange("p (b t) -> p b t", b=GB),
                                  chain_bank.rearrange("p (b t) -> p b t", b=GB),
                                  repeat(drive_tab[:, :], 1, GB), ALU.mult).then_inc(s_drive, 1)
                dve.wait_ge(s_drive, g + 1)
                link(dve.tensor_tensor_scan(modes[:, g, :], decay[:, :, :].rearrange("p b t -> p (b t)"),
                                            drive[:, g, :], 0.0, ALU.mult, ALU.add))
                for r in range(2):
                    ins = dve.tensor_tensor(turned[:, g, r, :].rearrange("p (b t) -> p b t", b=GB),
                                            modes[:, g, :].rearrange("p (b t) -> p b t", b=GB),
                                            repeat(turn_tab[:, r, :], 1, GB), ALU.mult)
                ins.then_inc(s_turned, 1)

            def residual(g):
                dve.wait_ge(s_y, g + 1)
                dve.tensor_tensor(h_b[:, g, :, :].rearrange("p b d -> p (b d)"),
                                  h_a[:, g, :, :].rearrange("p b d -> p (b d)"),
                                  chain_bank[:, 0:GB * D], ALU.add).then_inc(s_hb, 1)

            def norm_b(g):
                dve.wait_ge(s_hb, g + 1)
                norm(1, g, h_b)

            def route(g):
                dve.wait_ge(s_logit, g + 1)
                dve.tensor_tensor(logits[:, g, :, :], logit_bank[:, 0:GB * NE].rearrange("p (b e) -> p b e", b=GB),
                                  repeat(col("bg"), 1, GB), ALU.add).then_inc(s_lread, 1)
                dve.wait_ge(s_lread, g + 1)
                link(dve.tensor_reduce(top[:, g, :], logits[:, g, :, :], mybir.AxisListType.X, ALU.max))
                dve.tensor_tensor(below[:, g, :, :], logits[:, g, :, :],
                                  repeat(top[:, g, :], 2, NE), ALU.subtract).then_inc(s_below, 1)
                dve.wait_ge(s_below, g + 1)
                link(dve.tensor_scalar(chosen[:, g, :, :], below[:, g, :, :], 0.0, None, ALU.is_ge))

            def pick(g, h):
                if g == 0 and h == 0:
                    dve.wait_ge(s_bd_split, 1)
                dve.wait_ge(s_exp_mm, 2 * g + h + 1)
                for e in reversed(range(NE)):
                    ins = dve.copy_predicated(
                        picked[:, g, :, :].rearrange("p (b h) d -> p h b d", h=2)[:, h],
                        repeat(chosen[:, g, 2 * h:2 * h + 2, e], 2, D),
                        pair[h][:, :, e * D:(e + 1) * D])
                    if e:
                        link(ins)
                ins.then_inc(s_pick, 1)

            for i in range(STEPS):
                if on(i - 1):
                    norm_a(i - 1)
                if on(i - 3):
                    route(i - 3)
                if i == G + 2:
                    dve.wait_ge(s_expl, 1)
                    link(dve.tensor_reduce(denom[:, :, :].rearrange("p g b -> p (g b)"),
                                           expl[:, :, :, :].rearrange("p g b e -> p (g b) e"),
                                           mybir.AxisListType.X, ALU.add))
                    dve.reciprocal(prob[:, :, :], denom[:, :, :]).then_inc(s_prob, 1)
                if on(i - 1):
                    recurrence(i - 1)
                if on(i - 2):
                    norm_b(i - 2)
                if on(i - 4):
                    pick(i - 4, 0)
                if on(i):
                    product(i)
                if on(i - 1):
                    residual(i - 1)
                if on(i - 4):
                    pick(i - 4, 1)

        @block.tensor
        def _(pe):
            pe.wait_ge(s_emb_split, 1)
            pe.wait_ge(s_onehot, 1)
            for g in range(G):
                for b in range(GB):
                    for part in range(3):
                        mm = pe.matmul(bank[4 + g][:, b * (D + NL):(b + 1) * (D + NL)],
                                       onehot[0:V, g * GB + b, 3:3 + P], embp[part][:, :],
                                       start=(part == 0), stop=(part == 2))
                mm.then_inc(s_emb_mm, 1)
            pe.wait_ge(s_w1_split, 1)
            for g in range(G):
                n = 0
                for part in range(3):
                    for j in range(4):
                        mm = pe.matmul(bank[g], w1p[part][:, j, :],
                                       onehot[:, g * GB:(g + 1) * GB, 2 * j:2 * j + P],
                                       start=(n == 0), stop=(n == 11))
                        n += 1
                mm.then_inc(s_conv1, 1)
            pe.wait_ge(ld["w2"], 16)
            for q in range(G // 2):
                for r in range(2):
                    g = 2 * q + r
                    pe.wait_ge(s_h1, g + 1)
                    for k in range(K2):
                        mm = pe.matmul(bank[2 * q][r * D:(r + 1) * D, :], w2_sb[:, k, :],
                                       h1[:, g * GB:(g + 1) * GB, k:k + P],
                                       start=(k == 0), stop=(k == K2 - 1))
                mm.then_inc(s_conv2, 1)
            for q in range(G // 2):
                pe.wait_ge(s_h2, q + 1)
                for b in range(GB):
                    c = (q * GB + b) * 2 * K3
                    mm = pe.matmul(bank[1][:, c:c + 2 * K3], h2[:, q, b, :], col("w3"), start=True, stop=True)
            mm.then_inc(s_taps_mm, 1)
            pe.wait_ge(s_taps, 1)
            for k in range(K3):
                mm = pe.matmul(bank[3][:, 0:NB], shift(k), taps[:, :, k],
                               start=(k == 0), stop=(k == K3 - 1))
            mm.then_inc(s_ctx_mm, 1)

            def field(g):
                pe.wait_ge(s_amps, g + 1)
                pe.wait_ge(s_basis, g + 1)
                for b in range(GB):
                    mm = pe.matmul(bank[g][:, b * D:(b + 1) * D], basis[:, g, b * P:(b + 1) * P],
                                   amps[:, g * GB + b, :], start=True, stop=True)
                mm.then_inc(s_field, 1)

            def turn(n, g):
                pe.wait_ge(s_normed[n], g + 1)
                if n == 0 and g:
                    pe.wait_ge(s_hb, g)
                if n == 1 and g:
                    pe.wait_ge(s_H, KH * g)
                for c in range(2):
                    mm = pe.transpose((chain_bank, bank[6])[n][:, c * P:(c + 1) * P],
                                      normed[n][:, g, 2 * c:2 * c + 2, :].rearrange("p b d -> p (b d)"), identity)
                mm.then_inc(s_turn[n], 1)

            def inputs_in(g):
                if g == 0:
                    pe.wait_ge(ld["state"], 16)
                pe.wait_ge(s_xT[0], g + 1)
                for h in range(2):
                    rows = slice(h * D, (h + 1) * D)
                    mm = pe.matmul(chain_bank[:, h * 2 * P:(h + 1) * 2 * P], B_dup[rows, :],
                                   xT[rows, g].rearrange("p b t -> p (b t)"), start=True, stop=True)
                    mm.then_inc(s_v, 1)
                    if h == 0:
                        pe.wait_ge(s_v, 2 * g + 1)

            def outputs(g):
                if g == 0:
                    pe.wait_ge(s_tables, 1)
                pe.wait_ge(s_turned, g + 1)
                for j in range(GB):
                    b = 2 * (j % 2) + j // 2
                    for r, c in ((0, C_re), (1, neg_C_im[:, :])):
                        mm = pe.matmul(chain_bank[:, b * D:(b + 1) * D], turned[:, g, r, j * P:(j + 1) * P], c,
                                       start=(r == 0), stop=(r == 1))
                mm.then_inc(s_y, 1)

            def hidden(g):
                pe.wait_ge(s_xT[1], g + 1)
                for k in range(KH):
                    for h in range(2):
                        rows = slice(h * D, (h + 1) * D)
                        mm = pe.matmul(hid_pair[:, h, k * 2 * P:(k + 1) * 2 * P], W1[rows, k * P:(k + 1) * P],
                                       x2T[rows, g].rearrange("p b t -> p (b t)"), start=True, stop=True)
                mm.then_inc(s_hid, 1)

            def gate(g):
                pe.wait_ge(s_H, KH * (g + 1))
                if g:
                    pe.wait_ge(s_lread, g)
                for j in range(GB):
                    for k in range(KH):
                        mm = pe.matmul(logit_bank[:, j * NE:(j + 1) * NE], H[:, g, k, j * P:(j + 1) * P], Wg[:, k, :],
                                       start=(k == 0), stop=(k == KH - 1))
                mm.then_inc(s_logit, 1)

            def experts(g, h):
                if g == 0 and h == 0:
                    pe.wait_ge(ld["wd"], 16)
                    pe.wait_ge(s_bd_split, 1)
                    pe.wait_ge(s_ha, G)
                if g:
                    pe.wait_ge(s_pick, 2 * (g - 1) + h + 1)
                for jj in range(2):
                    j = 2 * h + jj
                    for k in range(KH):
                        pe.matmul(pair[h][:, jj, :], H[:, g, k, j * P:(j + 1) * P], wd_sb[:, k, :],
                                  start=(k == 0), stop=False)
                    mm = pe.matmul(pair[h][:, jj, :], ones[:, :], bdp[:, :], start=False, stop=True)
                mm.then_inc(s_exp_mm, 1)

            for i in range(STEPS):
                if on(i - 1):
                    turn(0, i - 1)
                    inputs_in(i - 1)
                if on(i - 3):
                    gate(i - 3)
                if on(i - 4):
                    experts(i - 4, 0)
                if on(i - 1):
                    outputs(i - 1)
                if on(i - 2):
                    turn(1, i - 2)
                    hidden(i - 2)
                if on(i):
                    field(i)
                if on(i - 4):
                    experts(i - 4, 1)



def _pack(table, width, **parts):
    out = np.zeros((P, width), np.float32)
    for name, a in parts.items():
        out[0:a.shape[0], table[name]] = a.reshape(a.shape[0], -1)
    return out


def _rows(a):
    return np.broadcast_to(a.reshape(1, -1), (P, a.size))


def kernel(x, fside_BS_continuous_positions, L0_tok_emb, L0_tok_locality_shapes, L0_tok_w1, L0_tok_b1,
           L0_tok_w2, L0_tok_b2, L0_tok_w3, L0_tok_b3, L0_tok_multiscale_widths, L0_tok_scale_weights,
           L0_attn_log_lambda_real, L0_attn_lambda_imag, L0_attn_log_dt, L0_attn_B, L0_attn_C_real,
           L0_attn_C_imag, L0_ffn_W1, L0_ffn_b1, L0_ffn_Wg, L0_ffn_bg, L0_ffn_Wd, L0_ffn_bd):
    import concourse.bacc as bacc
    from concourse.bass_utils import run_bass_kernel_spmd

    a = {k: np.asarray(v) for k, v in locals().items() if k[0:3] in ("L0_", "fsi") or k == "x"}
    twice = lambda v: np.concatenate([v, v], axis=0)

    line = np.arange(P)
    shift = np.zeros((P, P + 2), np.float32)
    shift[line, line + 1] = 1
    w3 = a["L0_tok_w3"][0]
    w3_both = np.zeros((2, D, 2, K3), np.float32)
    w3_both[0, :, 0], w3_both[1, :, 1] = w3, w3
    small = _pack(
        SMALL, NSMALL, shift=shift,
        half0=(line < D).astype(np.float32)[:, None], half1=(line >= D).astype(np.float32)[:, None],
        value=(line % V).astype(np.float32)[:, None],
        place=(line.astype(np.float32) / np.float32(P - 1))[:, None],
        emb=np.concatenate([a["L0_tok_emb"], a["L0_tok_locality_shapes"]], axis=1),
        b1=a["L0_tok_b1"][:, None], b2=twice(a["L0_tok_b2"])[:, None], b3=_rows(a["L0_tok_b3"]),
        widths=_rows(a["L0_tok_multiscale_widths"]), weights=_rows(a["L0_tok_scale_weights"]),
        log_re=twice(a["L0_attn_log_lambda_real"])[:, None], im=twice(a["L0_attn_lambda_imag"])[:, None],
        log_dt=twice(a["L0_attn_log_dt"])[:, None], w3=w3_both.reshape(2 * D, 2 * K3),
        ffn_b1=a["L0_ffn_b1"].reshape(KH, P).T, bg=_rows(a["L0_ffn_bg"]))
    w1 = np.zeros((2, V, 4, C1), np.float32)
    for k in range(K1):
        w1[k % 2, :, k // 2, :] = a["L0_tok_w1"][:, :, k].T
    w2 = a["L0_tok_w2"].transpose(1, 2, 0)
    B = twice(a["L0_attn_B"].T)
    state = _pack(
        STATE, NSTATE, B=np.concatenate([B, B], axis=1), C_re=twice(a["L0_attn_C_real"].T),
        C_im=twice(a["L0_attn_C_imag"].T), W1=twice(a["L0_ffn_W1"]),
        Wg=a["L0_ffn_Wg"].reshape(KH, P, NE).transpose(1, 0, 2))
    wd = a["L0_ffn_Wd"].reshape(NE, KH, P, D).transpose(2, 1, 0, 3).reshape(P, KH, NE * D)
    bd = np.zeros((96, NE * D), np.float32)
    bd[0], bd[32], bd[64] = (a["L0_ffn_bd"].reshape(-1),) * 3

    arrays = {"x": a["x"], "positions": a["fside_BS_continuous_positions"], "small": small,
              "w1": w1.reshape(P, 4, C1), "w2": w2, "state": state, "wd": wd, "bd": bd}
    arrays = {k: np.ascontiguousarray(v) for k, v in arrays.items()}

    nc = bacc.Bacc("TRN2", target_bir_lowering=False, num_devices=1)
    ins = [nc.dram_tensor(n, v.shape, mybir.dt.from_np(v.dtype), kind="ExternalInput").ap()
           for n, v in arrays.items()]
    out = nc.dram_tensor("out", (NB, P, D), F32, kind="ExternalOutput").ap()
    tower(nc, *ins, out)
    r = run_bass_kernel_spmd(nc, [arrays], core_ids=[0])
    return r.results[0]["out"]
```

```python
from contextlib import ExitStack

import concourse.bass as bass
import numpy as np
from concourse import mybir

ALU = mybir.AluOpType
ACT = mybir.ActivationFunctionType
F32 = mybir.dt.float32
BF16 = mybir.dt.bfloat16
I32 = mybir.dt.int32

P = 128
NB = 16
G = 4
GB = NB // G
T = GB * P
D = 64
V = 64
NL = 4
NS = 4
C1 = 128
K1, K2, K3 = 7, 5, 3
HID = 256
KH = HID // P
NE = 8
PADX = P + 6
PADH = P + 4
TURN = 2.0 ** 26
TURN_MASK = 0x3FFFFFC
PI_BELOW = 3.1415925
EPS = 1e-5
ON_PE = 2
ROUND = 1.5 * 2.0 ** 23


def columns(*parts):
    at, out = 0, {}
    for name, width in parts:
        out[name] = slice(at, at + width)
        at += width
    return out, at


SMALL, NSMALL = columns(
    ("shift", P + 2), ("half0", 1), ("half1", 1), ("value", 1), ("place", 1), ("emb", D + NL),
    ("b1", 1), ("b2", 1), ("b3", 1), ("widths", NS), ("weights", NS),
    ("log_re", 1), ("im", 1), ("log_dt", 1), ("w3", 2 * K3), ("ffn_b1", KH), ("bg", NE))
STATE, NSTATE = columns(("B", 2 * P), ("C_re", D), ("C_im", D), ("W1", HID), ("Wg", KH * NE))


def repeat(ap, axis, n):
    ap = ap.unsqueeze(axis)
    shape = list(ap.shape)
    shape[axis] = n
    return ap.broadcast_to(shape)


def tower(nc, x, positions, small, w1, w2, state, wd, bd, out):
    ctx = ExitStack()
    with ctx:
        def sb(name, shape, dt=F32):
            return ctx.enter_context(nc.sbuf_tensor(name, shape, dt))

        def sem(name):
            return ctx.enter_context(nc.semaphore(name))

        pair = [ctx.enter_context(nc.psum_tensor(f"pair{i}", [P, 2, T], F32)) for i in range(2)]
        bank = [pair[i // 2][:, i % 2, :] for i in range(4)]
        bank += [ctx.enter_context(nc.psum_tensor(f"bank{i}", [P, T], F32))[:, :] for i in range(4, 6)]
        state_bank, layer_bank = bank[4], bank[5]
        hid_pair = ctx.enter_context(nc.psum_tensor("hid_pair", [P, 2, T], F32))
        bank += [hid_pair[:, i, :] for i in range(2)]
        turn_bank = (state_bank[:, 0:2 * P], bank[7][:, 0:2 * P])
        logit_bank = bank[6]

        sm = sb("sm", [P, NSMALL])
        w1_sb = sb("w1_sb", [P, 4, C1])
        w2_sb = sb("w2_sb", [P, K2, D])
        st_sb = sb("st_sb", [P, NSTATE])
        wd_sb = sb("wd_sb", [P, KH, NE * D])
        bd_sb = sb("bd_sb", [96, NE * D])
        posb = sb("posb", [P, NB, P])
        bytes_pad = sb("bytes_pad", [P, NB, PADX], I32)

        def col(name):
            return sm[:, SMALL[name]]

        identity = sm[:, SMALL["shift"].start + 1:SMALL["shift"].start + 1 + P]

        def shift(k):
            return sm[:, SMALL["shift"].start + k:SMALL["shift"].start + k + P]

        B_rows = [st_sb[:, STATE["B"].start + h * P:STATE["B"].start + (h + 1) * P] for h in range(2)]
        C_re = st_sb[:, STATE["C_re"]]
        W1 = st_sb[:, STATE["W1"]]
        Wg = st_sb[:, STATE["Wg"]].rearrange("p (k e) -> p k e", k=KH)

        onehot = sb("onehot", [P, NB, PADX], BF16)
        embp = [sb(f"embp{i}", [V, D + NL], BF16) for i in range(3)]
        embr = [sb(f"embr{i}", [V, D + NL]) for i in range(2)]
        w1p = [sb(f"w1p{i}", [P, 4, C1], BF16) for i in range(3)]
        w1r = [sb(f"w1r{i}", [P, 4, C1]) for i in range(2)]
        bdp = sb("bdp", [96, NE * D], BF16)
        bdh = [sb(f"bdh{i}", [96, NE * D], BF16) for i in range(3)]
        bdr = [sb(f"bdr{i}", [96, NE * D]) for i in range(2)]
        ones = sb("ones", [96, P], BF16)
        shapes = sb("shapes", [P, NB, NL])
        h1 = sb("h1", [P, NB, PADH])
        h2 = sb("h2", [P, G // 2, GB, P])
        taps = sb("taps", [P, NB, K3])
        neg_b3 = sb("neg_b3", [P, 1])
        ctx_exp = sb("ctx_exp", [P, NB])
        amp_exp = sb("amp_exp", [P, NB])
        amp_tmp = sb("amp_tmp", [P, 3, NB])
        gain = sb("gain", [P, NB])
        amps = sb("amps", [P, NB, D])
        center = sb("center", [P, NB])
        absw = sb("absw", [P, NB])
        inv_width = sb("inv_width", [P, G, NS, GB])
        width = sb("width", [P, G, NS, GB])
        phase_tmp = sb("phase_tmp", [P, 3, NB])
        phase = sb("phase", [P, G, NS, GB])
        scale_w = sb("scale_w", [P, NS])
        dist = sb("dist", [P, NB, P])
        picked = posb[:, 0:8, :].rearrange("p b t -> p (b t)").rearrange("p (g b d) -> p g b d", g=G, b=GB)
        wave = sb("wave", [P, G, NS * T])
        angle = sb("angle", [P, G, NS * T], I32)
        bell = sb("bell", [P, G, NS * T])
        basis = sb("basis", [P, G, T])
        neg_pi = sb("neg_pi", [P, 1])
        minus_half = sb("minus_half", [P, NB])

        h_a = sb("h_a", [P, G, GB, D])
        h_b = sb("h_b", [P, G, GB, D])
        stats = sb("stats", [P, 2, G, GB, 6])
        mean_var = sb("mean_var", [P, 2, G, GB, 2])
        var_eps = sb("var_eps", [P, 2, G, GB])
        negated = sb("negated", [P, 2, G, GB])
        rstd = sb("rstd", [P, 2, G, GB])
        offset = sb("offset", [P, 2, G, GB])
        turned = wave[:, :, 0:2 * T].rearrange("p g (r t) -> p g r t", r=2)
        drive = wave[:, :, 2 * T:3 * T]
        modes = wave[:, :, 3 * T:4 * T]
        spent = angle[:, :, :].bitcast(F32)
        W = GB * D

        def spent_rows(k):
            return spent[:, :, k * W:(k + 1) * W].rearrange("p g (b d) -> p g b d", b=GB)

        normed = [spent_rows(0), spent_rows(1)]
        xT, x2T = (spent[:, :, k * W:(k + 1) * W].rearrange("p g (b t) -> p g b t", b=2) for k in (2, 3))
        scaled, result = spent_rows(4), spent_rows(5)
        H = bell[:, :, 0:KH * T].rearrange("p g (k t) -> p g k t", k=KH)
        neg_C_im = sb("neg_C_im", [P, D])
        spar = sb("spar", [P, 32])
        powers = sb("powers", [P, 2, P + 1])
        ptmp = sb("ptmp", [P, 4, P])
        drive_tab = sb("drive_tab", [P, P])
        turn_tab = sb("turn_tab", [P, 2, P])
        decay = sb("decay", [P, GB, P])
        logits = sb("logits", [P, G, GB, NE])
        top = sb("top", [P, G, GB])
        below = sb("below", [P, G, GB, NE])
        chosen = sb("chosen", [P, G, GB, NE], I32)
        expl = sb("expl", [P, G, GB, NE])
        denom = sb("denom", [P, G, GB])
        prob = sb("prob", [P, G, GB])

        ld = {n: sem(f"ld_{n}") for n in ("x", "pos", "small", "w1", "w2", "state", "wd", "bd")}
        stored = sem("stored")
        dve_chain, pool_chain = sem("dve_chain"), sem("pool_chain")
        s_pad = sem("s_pad")
        s_cst = sem("s_cst")
        s_emb_split = sem("s_emb_split")
        s_onehot = sem("s_onehot")
        s_w1_part, s_w1_left = sem("s_w1_part"), sem("s_w1_left")
        s_bd_part, s_bd_left = sem("s_bd_part"), sem("s_bd_left")
        s_dist, s_picked0 = sem("s_dist"), sem("s_picked0")
        s_copied = [sem("s_copied0"), sem("s_copied1")]
        s_bd_split = sem("s_bd_split")
        s_shapes_mm, s_shapes, s_emb_mm = sem("s_shapes_mm"), sem("s_shapes"), sem("s_emb_mm")
        s_conv1, s_h1 = sem("s_conv1"), sem("s_h1")
        s_conv2, s_h2 = sem("s_conv2"), sem("s_h2")
        s_taps_mm, s_taps = sem("s_taps_mm"), sem("s_taps")
        s_ctx_mm, s_ctx = sem("s_ctx_mm"), sem("s_ctx")
        s_amp_exp, s_negb3 = sem("s_amp_exp"), sem("s_negb3")
        s_gain, s_amps = sem("s_gain"), sem("s_amps")
        s_phase, s_ampden = sem("s_phase"), sem("s_ampden")
        s_z, s_z_pool, s_angle = sem("s_z"), sem("s_z_pool"), sem("s_angle")
        s_square, s_square_pool, s_bell, s_cos = sem("s_square"), sem("s_square_pool"), sem("s_bell"), sem("s_cos")
        s_prod, s_basis = sem("s_prod"), sem("s_basis")
        s_sexp, s_spar_neg = sem("s_sexp"), sem("s_spar_neg")
        s_tables = sem("s_tables")
        s_field, s_ha = sem("s_field"), sem("s_ha")
        s_mv = [sem("s_mv0"), sem("s_mv1")]
        s_rstd = [sem("s_rstd0"), sem("s_rstd1")]
        s_normed = [sem("s_normed0"), sem("s_normed1")]
        s_turn = [sem("s_turn0"), sem("s_turn1")]
        s_xT = [sem("s_xT0"), sem("s_xT1")]
        s_v, s_drive = sem("s_v"), sem("s_drive")
        s_turned = sem("s_turned")
        s_y, s_hb = sem("s_y"), sem("s_hb")
        s_hid, s_H = sem("s_hid"), sem("s_H")
        s_logit, s_lread, s_below = sem("s_logit"), sem("s_lread"), sem("s_below")
        s_expl, s_prob = sem("s_expl"), sem("s_prob")
        s_exp_mm = [sem("s_exp_mm0"), sem("s_exp_mm1")]
        s_result, s_last = sem("s_result"), sem("s_last")

        def widths_away(engine, g):
            return engine.tensor_tensor(
                wave[:, g, :].rearrange("p (s t) -> p s t", s=NS),
                repeat(dist[:, g * GB:(g + 1) * GB, :].rearrange("p b t -> p (b t)"), 1, NS),
                repeat(inv_width[:, g, :, :].rearrange("p s b -> p (s b)"), 2, P), ALU.mult)

        def z_is_there(engine, g):
            if g < G - 1:
                engine.wait_ge(s_z, g + 1)
            else:
                engine.wait_ge(s_z_pool, 1)

        block = ctx.enter_context(nc.Block())

        @block.sync
        def _(sp):
            sp.dma_start(sm[:, :], small).then_inc(ld["small"], 16)
            for half in range(2):
                rows = slice(half * V, half * V + V)
                sp.dma_start(bytes_pad[rows, :, 3 - half:3 - half + P], repeat(x, 0, V)).then_inc(ld["x"], 16)
            sp.dma_start(posb[:, :, :], repeat(positions, 0, P)).then_inc(ld["pos"], 16)
            sp.dma_start(w2_sb[:, :, :], w2).then_inc(ld["w2"], 16)
            sp.dma_start(st_sb[:, :], state).then_inc(ld["state"], 16)
            sp.dma_start(wd_sb[:, :, :], wd).then_inc(ld["wd"], 16)
            for g in range(G):
                if g < G - 1:
                    sp.wait_ge(s_result, g + 1)
                else:
                    sp.wait_ge(s_last, 1)
                sp.dma_start(out[g * GB:(g + 1) * GB].rearrange("b p d -> p b d"),
                             result[:, g]).then_inc(stored, 16)
            sp.wait_ge(stored, 16 * G)

        @block.gpsimd
        def _(pool):
            count = [0]

            def link(ins):
                count[0] += 1
                ins.then_inc(pool_chain, 1)
                pool.wait_ge(pool_chain, count[0])

            for half in range(2):
                rows = slice(half * V, half * V + V)
                for cols in (slice(0, 3 - half), slice(3 - half + P, PADX)):
                    pool.memset(bytes_pad[rows, :, cols], -1).then_inc(s_pad, 1)
                    pool.wait_ge(s_pad, 1 + 2 * half + (cols.start > 0))
            pool.memset(neg_pi[:, :], -PI_BELOW)
            pool.memset(h1[:, :, 0:2], 0.0)
            pool.memset(h1[:, :, 2 + P:], 0.0)
            pool.memset(ones[:, :], 1.0).then_inc(s_cst, 1)

            link(pool.memset(minus_half[:, :], -0.5))
            slot = iter(range(32))

            def new():
                k = next(slot)
                return spar[:, k:k + 1]

            lam, dt = new(), new()

            pool.wait_ge(s_sexp, 2)
            dtc, hr, hi = new(), new(), new()
            link(pool.tensor_scalar(dtc, dt, 0.005, 0.1, ALU.max, ALU.min))
            link(pool.tensor_tensor(hr, dtc, lam, ALU.mult))
            link(pool.tensor_scalar(hr, hr, -0.5, None, ALU.mult))
            link(pool.tensor_tensor(hi, dtc, col("im"), ALU.mult))
            link(pool.tensor_scalar(hi, hi, 0.5, None, ALU.mult))
            low, high, hi2, d2, n2, inv = new(), new(), new(), new(), new(), new()
            link(pool.tensor_scalar(low, hr, -1.0, 1.0, ALU.mult, ALU.add))
            link(pool.tensor_scalar(high, hr, 1.0, None, ALU.add))
            link(pool.tensor_tensor(hi2, hi, hi, ALU.mult))
            link(pool.tensor_tensor(d2, low, low, ALU.mult))
            link(pool.tensor_tensor(d2, d2, hi2, ALU.add))
            link(pool.tensor_tensor(n2, high, high, ALU.mult))
            link(pool.tensor_tensor(n2, n2, hi2, ALU.add))
            link(pool.tensor_tensor(inv, d2, minus_half[:, 0:1], ALU.pow))
            link(pool.tensor_tensor(inv, inv, inv, ALU.mult))
            rho2, rho, irho, zero = new(), new(), new(), new()
            link(pool.tensor_tensor(rho2, n2, inv, ALU.mult))
            link(pool.tensor_scalar(zero, rho2, 1e-30, None, ALU.is_lt))
            link(pool.tensor_scalar(rho, rho2, 1e-30, None, ALU.max))
            link(pool.tensor_tensor(irho, rho, minus_half[:, 0:1], ALU.pow))
            link(pool.tensor_tensor(rho, rho2, irho, ALU.mult))
            link(pool.tensor_tensor(irho, irho, inv, ALU.mult))
            keep, c1, s1 = new(), new(), new()
            link(pool.tensor_scalar(keep, zero, -1.0, 1.0, ALU.mult, ALU.add))
            link(pool.tensor_tensor(irho, irho, keep, ALU.mult))
            link(pool.tensor_tensor(c1, low, high, ALU.mult))
            link(pool.tensor_tensor(c1, c1, hi2, ALU.subtract))
            link(pool.tensor_tensor(c1, c1, irho, ALU.mult))
            link(pool.tensor_tensor(powers[:, 0, 1:2], c1, zero, ALU.add))
            link(pool.tensor_scalar(s1, hi, 2.0, None, ALU.mult))
            link(pool.tensor_tensor(powers[:, 1, 1:2], s1, irho, ALU.mult))
            link(pool.memset(powers[:, 0, 0:1], 1.0))
            link(pool.memset(powers[:, 1, 0:1], 0.0))
            m = 1
            while m < P:
                c, s = powers[:, 0, m:m + 1], powers[:, 1, m:m + 1]
                link(pool.tensor_scalar(ptmp[:, 0:2, 0:m], powers[:, :, 1:m + 1], c, None, ALU.mult))
                link(pool.tensor_scalar(ptmp[:, 2:4, 0:m], powers[:, :, 1:m + 1], s, None, ALU.mult))
                link(pool.tensor_tensor(powers[:, 0, m + 1:2 * m + 1], ptmp[:, 0, 0:m], ptmp[:, 3, 0:m],
                                        ALU.subtract))
                link(pool.tensor_tensor(powers[:, 1, m + 1:2 * m + 1], ptmp[:, 1, 0:m], ptmp[:, 2, 0:m],
                                        ALU.add))
                m *= 2
            pool.wait_ge(s_dist, 1)
            widths_away(pool, G - 1).then_inc(s_z_pool, 1)
            pool.wait_ge(s_z, 3)
            pool.tensor_tensor(bell[:, 2, :], wave[:, 2, :], wave[:, 2, :], ALU.mult).then_inc(s_square_pool, 1)
            b_re, b_im, mix_c, mix_s, t0 = new(), new(), new(), new(), new()
            link(pool.tensor_tensor(t0, dtc, inv, ALU.mult))
            link(pool.tensor_tensor(b_re, t0, low, ALU.mult))
            link(pool.tensor_tensor(b_im, t0, hi, ALU.mult))
            link(pool.tensor_tensor(mix_c, b_re, col("half0"), ALU.mult))
            link(pool.tensor_tensor(t0, b_im, col("half1"), ALU.mult))
            link(pool.tensor_tensor(mix_c, mix_c, t0, ALU.add))
            link(pool.tensor_tensor(mix_s, b_im, col("half0"), ALU.mult))
            link(pool.tensor_tensor(t0, b_re, col("half1"), ALU.mult))
            link(pool.tensor_tensor(mix_s, mix_s, t0, ALU.subtract))
            cos_t, sin_t = powers[:, 0, 0:P], powers[:, 1, 0:P]
            link(pool.tensor_scalar(ptmp[:, 0, :], cos_t, mix_c, None, ALU.mult))
            link(pool.tensor_scalar(ptmp[:, 1, :], sin_t, mix_s, None, ALU.mult))
            link(pool.tensor_tensor(drive_tab[:, :], ptmp[:, 0, :], ptmp[:, 1, :], ALU.add))
            link(pool.tensor_scalar(ptmp[:, 0, :], cos_t, col("half0"), None, ALU.mult))
            link(pool.tensor_scalar(ptmp[:, 1, :], sin_t, col("half1"), None, ALU.mult))
            link(pool.tensor_tensor(turn_tab[:, 0, :], ptmp[:, 0, :], ptmp[:, 1, :], ALU.subtract))
            link(pool.tensor_scalar(ptmp[:, 2, :], sin_t, col("half0"), None, ALU.mult))
            link(pool.tensor_scalar(ptmp[:, 3, :], cos_t, col("half1"), None, ALU.mult))
            link(pool.tensor_tensor(turn_tab[:, 1, :], ptmp[:, 2, :], ptmp[:, 3, :], ALU.add))
            link(pool.memset(decay[:, :, :], 1.0))
            link(pool.tensor_scalar(decay[:, :, :], decay[:, :, :], rho, None, ALU.mult))
            link(pool.memset(decay[:, :, 0:1], 0.0))
            pool.wait_ge(ld["state"], 16)
            pool.tensor_scalar(neg_C_im[:, :], st_sb[:, STATE["C_im"]], -1.0, None, ALU.mult).then_inc(s_tables, 1)

            pool.memset(picked[:, :, :, :], 0.0).then_inc(s_picked0, 1)

            def sum_scales(g):
                pool.wait_ge(s_prod, NS * (g + 1))
                w = bell[:, g, :].rearrange("p (s t) -> p s t", s=NS)
                link(pool.tensor_tensor(w[:, 0:2, :], w[:, 0:2, :], w[:, 2:4, :], ALU.add))
                pool.tensor_tensor(basis[:, g, :], w[:, 0, :], w[:, 1, :], ALU.add).then_inc(s_basis, 1)

            def inv_std(n, g):
                pool.wait_ge(s_mv[n], g + 1)
                link(pool.tensor_scalar(var_eps[:, n, g, :], mean_var[:, n, g, :, 1], EPS, None, ALU.add))
                pool.tensor_scalar(negated[:, n, g, :], mean_var[:, n, g, :, 0], -1.0, None, ALU.mult)
                link(pool.tensor_tensor(rstd[:, n, g, :], var_eps[:, n, g, :], minus_half[:, 0:GB], ALU.pow))
                pool.tensor_tensor(offset[:, n, g, :], negated[:, n, g, :], rstd[:, n, g, :],
                                   ALU.mult).then_inc(s_rstd[n], 1)

            def finish(g):
                if g == 0:
                    pool.wait_ge(s_prob, 1)
                for h in range(2):
                    pool.wait_ge(s_copied[h], NE * (g + 1))
                link(pool.tensor_tensor(
                    scaled[:, g].rearrange("p (b h) d -> p b h d", h=2),
                    picked[:, g].rearrange("p (b h) d -> p b h d", h=2),
                    repeat(prob[:, g].rearrange("p (h b) -> p b h", h=2), 3, D), ALU.mult))
                pool.tensor_tensor(result[:, g], scaled[:, g], h_b[:, g], ALU.add).then_inc(s_result, 1)

            inv_std(0, 0)
            sum_scales(2)
            inv_std(0, 1)
            inv_std(1, 0)
            sum_scales(3)
            inv_std(0, 2)
            inv_std(1, 1)
            inv_std(0, 3)
            inv_std(1, 2)
            inv_std(1, 3)
            for g in range(G - 1):
                finish(g)

        @block.scalar
        def _(act):
            act.dma_start(w1_sb[:, :, :], w1).then_inc(ld["w1"], 16)
            act.dma_start(bd_sb[:, :], bd).then_inc(ld["bd"], 16)
            act.wait_ge(ld["small"], 16)
            act.activation(spar[:, 0:1], col("log_re"), ACT.Exp).then_inc(s_sexp, 1)
            act.activation(spar[:, 1:2], col("log_dt"), ACT.Exp).then_inc(s_sexp, 1)
            act.activation(neg_b3[:, :], col("b3"), ACT.Copy, scale=-1.0).then_inc(s_negb3, 1)
            act.wait_ge(ld["w1"], 16)
            for k in range(3):
                if k:
                    act.wait_ge(s_w1_left, k)
                act.copy(w1p[k][:], w1_sb[:] if k == 0 else w1r[k - 1][:]).then_inc(s_w1_part, 1)
                if k:
                    act.wait_ge(s_bd_left, k)
                else:
                    act.wait_ge(ld["bd"], 16)
                act.copy(bdh[k][:], bd_sb[:] if k == 0 else bdr[k - 1][:]).then_inc(s_bd_part, 1)
            act.wait_ge(s_shapes_mm, 1)
            act.copy(shapes[:, :, :].rearrange("p b c -> p (b c)"), bank[4][:, 0:NB * NL]).then_inc(s_shapes, 1)
            act.wait_ge(s_shapes, 1)
            act.activation(amp_exp[:, :], shapes[:, :, 2], ACT.Exp, scale=-1.0).then_inc(s_amp_exp, 1)

            def conv1_out(g):
                act.wait_ge(s_conv1, g + 1)
                act.activation(h1[:, g * GB:(g + 1) * GB, 2:2 + P],
                               bank[g].rearrange("p (b s) -> p b s", b=GB), ACT.Gelu,
                               bias=col("b1")).then_inc(s_h1, 1)

            def square(g):
                z_is_there(act, g)
                act.activation(bell[:, g, :], wave[:, g, :], ACT.Square).then_inc(s_square, 1)

            def square_is_there(g):
                if g == 2:
                    act.wait_ge(s_square_pool, 1)
                else:
                    act.wait_ge(s_square, min(g + 1, G - 1))

            def gaussian(g):
                square_is_there(g)
                act.activation(bell[:, g, :], bell[:, g, :], ACT.Exp, scale=-0.5).then_inc(s_bell, 1)

            def cosine(g):
                act.wait_ge(s_angle, g + 1)
                square_is_there(g)
                act.activation(wave[:, g, :], angle[:, g, :], ACT.Sin, bias=neg_pi[:, 0:1],
                               scale=2.0 * PI_BELOW / TURN).then_inc(s_cos, 1)

            act.wait_ge(s_cst, 1)
            conv1_out(0)
            square(0)
            conv1_out(1)
            conv1_out(2)
            square(1)
            conv1_out(3)
            gaussian(0)
            gaussian(1)
            for q in range(G // 2):
                act.wait_ge(s_conv2, q + 1)
                act.activation(h2[:, q, :, :].rearrange("p b s -> p (b s)"), bank[2 * q], ACT.Gelu,
                               bias=col("b2")).then_inc(s_h2, 1)
            cosine(0)
            act.wait_ge(s_taps_mm, 1)
            act.copy(taps[:, :, :].rearrange("p b k -> p (b k)"), bank[1][:, 0:NB * K3]).then_inc(s_taps, 1)
            cosine(1)
            act.wait_ge(s_ctx_mm, 1)
            act.wait_ge(s_negb3, 1)
            act.activation(ctx_exp[:, :], bank[3][:, 0:NB], ACT.Exp, bias=neg_b3[:, 0:1],
                           scale=-1.0).then_inc(s_ctx, 1)
            gaussian(2)
            square(3)
            gaussian(3)

            def field_out(g):
                act.wait_ge(s_field, g + 1)
                act.copy(h_a[:, g, :, :].rearrange("p b d -> p (b d)"), bank[g][:, 0:GB * D]).then_inc(s_ha, 1)

            def transposed_out(n, g):
                act.wait_ge(s_turn[n], g + 1)
                act.copy((xT, x2T)[n][:, g].rearrange("p b t -> p (b t)"), turn_bank[n]).then_inc(s_xT[n], 1)

            def normalise(n, g):
                act.wait_ge(s_rstd[n], g + 1)
                for b in range(GB):
                    ins = act.activation(normed[n][:, g, b, :], (h_a, h_b)[n][:, g, b, :], ACT.Identity,
                                         scale=rstd[:, n, g, b:b + 1], bias=offset[:, n, g, b:b + 1])
                ins.then_inc(s_normed[n], 1)

            def hidden(g):
                act.wait_ge(s_hid, g + 1)
                for k in range(KH):
                    act.activation(H[:, g, k, :].rearrange("p (h t) -> p h t", h=2),
                                   hid_pair[:, :, k * 2 * P:(k + 1) * 2 * P], ACT.Gelu,
                                   bias=sm[:, SMALL["ffn_b1"].start + k:SMALL["ffn_b1"].start + k + 1]).then_inc(s_H, 1)

            field_out(0)
            cosine(2)
            normalise(0, 0)
            field_out(1)
            transposed_out(0, 0)
            cosine(3)
            normalise(0, 1)
            transposed_out(0, 1)
            normalise(1, 0)
            field_out(2)
            transposed_out(1, 0)
            hidden(0)
            normalise(0, 2)
            normalise(1, 1)
            field_out(3)
            transposed_out(0, 2)
            transposed_out(1, 1)
            normalise(0, 3)
            transposed_out(0, 3)
            hidden(1)
            normalise(1, 2)
            transposed_out(1, 2)
            hidden(2)
            normalise(1, 3)
            transposed_out(1, 3)
            hidden(3)
            act.wait_ge(s_below, G)
            act.activation(expl[:, :, :, :], below[:, :, :, :], ACT.Exp).then_inc(s_expl, 1)

        @block.vector
        def _(dve):
            count = [0]

            def link(ins):
                count[0] += 1
                ins.then_inc(dve_chain, 1)
                dve.wait_ge(dve_chain, count[0])

            dve.wait_ge(ld["small"], 16)
            table = sm[0:V, SMALL["emb"]]
            link(dve.tensor_copy(embp[0][:], table))
            link(dve.tensor_tensor(embr[0][:], table, embp[0][:], ALU.subtract))
            link(dve.tensor_copy(embp[1][:], embr[0][:]))
            link(dve.tensor_tensor(embr[1][:], embr[0][:], embp[1][:], ALU.subtract))
            dve.tensor_copy(embp[2][:], embr[1][:]).then_inc(s_emb_split, 1)
            link(dve.tensor_tensor(scale_w[:, :], col("weights"), col("weights"), ALU.mult))

            def left(part, whole, rest, s_part, s_left):
                for k in range(2):
                    dve.wait_ge(s_part, k + 1)
                    dve.tensor_tensor(rest[k][:], (whole if k == 0 else rest[0])[:], part[k][:],
                                      ALU.subtract).then_inc(s_left, 1)

            left(w1p, w1_sb, w1r, s_w1_part, s_w1_left)
            dve.wait_ge(s_pad, 4)
            dve.wait_ge(ld["x"], 32)
            dve.tensor_scalar(onehot[:, :, :], bytes_pad[:, :, :], col("value"), None,
                              ALU.is_equal).then_inc(s_onehot, 1)
            left(bdh, bd_sb, bdr, s_bd_part, s_bd_left)
            for k in range(3):
                dve.wait_ge(s_bd_part, k + 1)
                dve.tensor_copy(bdp[32 * k:32 * k + 32, :], bdh[k][32 * k:32 * k + 32, :]).then_inc(s_bd_split, 1)

            dve.wait_ge(s_shapes, 1)
            lp = [shapes[:, :, k] for k in range(NL)]
            dve.tensor_scalar(center[:, :], lp[0], 0.05, col("place"), ALU.mult, ALU.add)
            dve.tensor_scalar(phase_tmp[:, 0, :], lp[3], 0.5, ROUND, ALU.mult, ALU.add)
            link(dve.scalar_tensor_tensor(out=absw[:, :], in0=lp[1], scalar=-1.0, in1=lp[1], op0=ALU.mult, op1=ALU.max))
            dve.tensor_scalar(phase_tmp[:, 1, :], phase_tmp[:, 0, :], -ROUND, None, ALU.add)
            for s in range(NS):
                c = SMALL["widths"].start + s
                ins = dve.tensor_scalar(width[:, :, s, :], absw[:, :].rearrange("p (g b) -> p g b", g=G),
                                        sm[:, c:c + 1], 1e-5, ALU.mult, ALU.add)
            link(ins)
            dve.scalar_tensor_tensor(out=phase_tmp[:, 2, :], in0=lp[3], scalar=0.5, in1=phase_tmp[:, 1, :],
                                     op0=ALU.mult, op1=ALU.subtract)
            link(dve.reciprocal(inv_width[:, :, :, :], width[:, :, :, :]))
            dve.tensor_scalar(phase[:, :, :, :],
                              repeat(phase_tmp[:, 2, :].rearrange("p (g b) -> p g b", g=G), 2, NS),
                              0.75, TURN, ALU.add, ALU.mult).then_inc(s_phase, 1)
            dve.wait_ge(ld["pos"], 16)
            dve.tensor_tensor(dist[:, :, :], posb[:, :, :], repeat(center[:, :], 2, P),
                              ALU.subtract).then_inc(s_dist, 1)
            dve.wait_ge(s_dist, 1)

            def z(g):
                widths_away(dve, g).then_inc(s_z, 1)

            def turns(g):
                z_is_there(dve, g)
                link(dve.scalar_tensor_tensor(
                    out=angle[:, g, :].rearrange("p (s t) -> p s t", t=P),
                    in0=wave[:, g, :].rearrange("p (s t) -> p s t", t=P), scalar=TURN,
                    in1=repeat(phase[:, g, :, :].rearrange("p s b -> p (s b)"), 2, P),
                    op0=ALU.mult, op1=ALU.add))
                dve.tensor_scalar(angle[:, g, :], angle[:, g, :], TURN_MASK, None,
                                  ALU.bitwise_and).then_inc(s_angle, 1)

            def gates():
                dve.wait_ge(s_ctx, 1)
                dve.wait_ge(s_ampden, 1)
                for q in range(2):
                    cols = slice(8 * q, 8 * q + 8)
                    ins = dve.scalar_tensor_tensor(
                        out=amp_tmp[:, 1, cols].rearrange("p (r b) -> p r b", r=2),
                        in0=ctx_exp[:, cols].rearrange("p (b r) -> p r b", r=2), scalar=1.0,
                        in1=amp_tmp[:, 0, cols].rearrange("p (r b) -> p r b", r=2), op0=ALU.add, op1=ALU.mult)
                link(ins)
                dve.reciprocal(gain[:, :], amp_tmp[:, 1, :]).then_inc(s_gain, 1)
                dve.wait_ge(s_gain, 1)
                for q in range(2):
                    b = slice(8 * q, 8 * q + 8)
                    dve.wait_ge(s_emb_mm, q + 1)
                    dve.tensor_tensor(amps[:, b, :], bank[4 + q].rearrange("p (b d) -> p b d", d=D),
                                      repeat(gain[:, b], 2, D), ALU.mult).then_inc(s_amps, 1)

            def product(g):
                dve.wait_ge(s_cos, g + 1)
                for s in range(NS):
                    part = slice(s * T, (s + 1) * T)
                    dve.scalar_tensor_tensor(out=bell[:, g, part], in0=bell[:, g, part],
                                             scalar=scale_w[:, s:s + 1], in1=wave[:, g, part],
                                             op0=ALU.mult, op1=ALU.mult).then_inc(s_prod, 1)

            def moments(n, g):
                if n == 0:
                    dve.wait_ge(s_ha, g + 1)
                for b in range(GB):
                    ins = dve.bn_stats(stats[:, n, g, b, :], (h_a, h_b)[n][:, g, b, :])
                link(ins)
                for b in range(GB):
                    ins = dve.bn_aggr(mean_var[:, n, g, b, :], stats[:, n, g, b, :])
                ins.then_inc(s_mv[n], 1)

            def recurrence(g):
                if g == 0:
                    dve.wait_ge(s_tables, 1)
                dve.wait_ge(s_v, g + 1)
                dve.tensor_tensor(drive[:, g, :].rearrange("p (b t) -> p b t", b=GB),
                                  state_bank.rearrange("p (b t) -> p b t", b=GB),
                                  repeat(drive_tab[:, :], 1, GB), ALU.mult).then_inc(s_drive, 1)
                dve.wait_ge(s_drive, g + 1)
                link(dve.tensor_tensor_scan(modes[:, g, :], decay[:, :, :].rearrange("p b t -> p (b t)"),
                                            drive[:, g, :], 0.0, ALU.mult, ALU.add))
                for r in range(2):
                    ins = dve.tensor_tensor(turned[:, g, r, :].rearrange("p (b t) -> p b t", b=GB),
                                            modes[:, g, :].rearrange("p (b t) -> p b t", b=GB),
                                            repeat(turn_tab[:, r, :], 1, GB), ALU.mult)
                ins.then_inc(s_turned, 1)

            def residual(g):
                dve.wait_ge(s_y, g + 1)
                dve.wait_ge(s_ha, g + 1)
                dve.tensor_tensor(h_b[:, g, :, :].rearrange("p b d -> p (b d)"),
                                  h_a[:, g, :, :].rearrange("p b d -> p (b d)"),
                                  layer_bank[:, 0:GB * D], ALU.add).then_inc(s_hb, 1)
                dve.wait_ge(s_hb, g + 1)
                moments(1, g)

            def route(g):
                dve.wait_ge(s_logit, g + 1)
                dve.tensor_tensor(logits[:, g, :, :], logit_bank[:, 0:GB * NE].rearrange("p (b e) -> p b e", b=GB),
                                  repeat(col("bg"), 1, GB), ALU.add).then_inc(s_lread, 1)
                dve.wait_ge(s_lread, g + 1)
                link(dve.tensor_reduce(top[:, g, :], logits[:, g, :, :], mybir.AxisListType.X, ALU.max))
                dve.tensor_tensor(below[:, g, :, :], logits[:, g, :, :],
                                  repeat(top[:, g, :], 2, NE), ALU.subtract).then_inc(s_below, 1)
                dve.wait_ge(s_below, g + 1)
                link(dve.tensor_scalar(chosen[:, g, :, :], below[:, g, :, :], 0.0, None, ALU.is_ge))

            def pick(g, *halves):
                if g == 0:
                    dve.wait_ge(s_picked0, 1)
                for e in reversed(range(NE)):
                    for h in halves:
                        if e == NE - 1:
                            dve.wait_ge(s_exp_mm[h], g + 1)
                        else:
                            dve.wait_ge(s_copied[h], NE * g + NE - 1 - e)
                        dve.copy_predicated(
                            picked[:, g, :, :].rearrange("p (b h) d -> p h b d", h=2)[:, h],
                            repeat(chosen[:, g, 2 * h:2 * h + 2, e], 2, D),
                            pair[h][:, :, e * D:(e + 1) * D]).then_inc(s_copied[h], 1)

            def probability():
                dve.wait_ge(s_expl, 1)
                link(dve.tensor_reduce(denom[:, :, :].rearrange("p g b -> p (g b)"),
                                       expl[:, :, :, :].rearrange("p g b e -> p (g b) e"),
                                       mybir.AxisListType.X, ALU.add))
                dve.reciprocal(prob[:, :, :], denom[:, :, :]).then_inc(s_prob, 1)

            def finish(g):
                dve.wait_ge(s_prob, 1)
                for h in range(2):
                    dve.wait_ge(s_copied[h], NE * (g + 1))
                link(dve.tensor_tensor(
                    scaled[:, g].rearrange("p (b h) d -> p b h d", h=2),
                    picked[:, g].rearrange("p (b h) d -> p b h d", h=2),
                    repeat(prob[:, g].rearrange("p (h b) -> p b h", h=2), 3, D), ALU.mult))
                dve.tensor_tensor(result[:, g], scaled[:, g], h_b[:, g], ALU.add).then_inc(s_last, 1)

            z(0)
            dve.wait_ge(s_phase, 1)
            turns(0)
            z(1)
            turns(1)
            z(2)
            turns(2)
            dve.wait_ge(s_amp_exp, 1)
            dve.tensor_scalar(amp_tmp[:, 0, :], amp_exp[:, :], 1.0, None, ALU.add).then_inc(s_ampden, 1)
            turns(3)
            product(0)
            gates()
            product(1)
            moments(0, 0)
            product(2)
            recurrence(0)
            moments(0, 1)
            residual(0)
            product(3)
            recurrence(1)
            moments(0, 2)
            residual(1)
            moments(0, 3)
            route(0)
            recurrence(2)
            pick(0, 1)
            pick(0, 0)
            residual(2)
            recurrence(3)
            route(1)
            residual(3)
            pick(1, 1)
            pick(1, 0)
            route(2)
            pick(2, 1)
            pick(2, 0)
            route(3)
            pick(3, 1)
            probability()
            pick(3, 0)
            finish(G - 1)

        @block.tensor
        def _(pe):
            pe.wait_ge(s_emb_split, 1)
            pe.wait_ge(s_onehot, 1)

            def look_up(where, b, cols):
                for part in range(3):
                    mm = pe.matmul(where, onehot[0:V, b, 3:3 + P], embp[part][:, cols],
                                   start=(part == 0), stop=(part == 2))
                return mm

            for b in range(NB):
                mm = look_up(bank[4][:, b * NL:(b + 1) * NL], b, slice(D, D + NL))
            mm.then_inc(s_shapes_mm, 1)
            pe.wait_ge(s_w1_part, 3)
            for g in range(G):
                n = 0
                for part in range(3):
                    for j in range(4):
                        mm = pe.matmul(bank[g], w1p[part][:, j, :],
                                       onehot[:, g * GB:(g + 1) * GB, 2 * j:2 * j + P],
                                       start=(n == 0), stop=(n == 11))
                        n += 1
                mm.then_inc(s_conv1, 1)
            pe.wait_ge(ld["w2"], 16)
            for q in range(G // 2):
                for r in range(2):
                    g = 2 * q + r
                    pe.wait_ge(s_h1, g + 1)
                    for k in range(K2):
                        mm = pe.matmul(bank[2 * q][r * D:(r + 1) * D, :], w2_sb[:, k, :],
                                       h1[:, g * GB:(g + 1) * GB, k:k + P],
                                       start=(k == 0), stop=(k == K2 - 1))
                mm.then_inc(s_conv2, 1)
            pe.wait_ge(s_shapes, 1)
            for q in range(2):
                for b in range(8):
                    mm = look_up(bank[4 + q][:, b * D:(b + 1) * D], 8 * q + b, slice(0, D))
                mm.then_inc(s_emb_mm, 1)
            def keep_warm(n):
                for _ in range(n):
                    pe.matmul(hid_pair[:, 1, :], w1p[0][:, 0, :], onehot[:, 0:GB, 0:P], start=True, stop=True)

            for q in range(G // 2):
                pe.wait_ge(s_h2, q + 1)
                for b in range(GB):
                    c = (q * GB + b) * 2 * K3
                    mm = pe.matmul(bank[1][:, c:c + 2 * K3], h2[:, q, b, :], col("w3"), start=True, stop=True)
            mm.then_inc(s_taps_mm, 1)
            keep_warm(4)
            pe.wait_ge(s_taps, 1)
            for k in range(K3):
                mm = pe.matmul(bank[3][:, 0:NB], shift(k), taps[:, :, k],
                               start=(k == 0), stop=(k == K3 - 1))
            mm.then_inc(s_ctx_mm, 1)

            def field(g):
                pe.wait_ge(s_amps, g // 2 + 1)
                if g < ON_PE:
                    for s in range(NS):
                        pe.wait_ge(s_prod, NS * g + s + 1)
                        for b in range(GB):
                            c = s * T + b * P
                            mm = pe.matmul(bank[g][:, b * D:(b + 1) * D], bell[:, g, c:c + P],
                                           amps[:, g * GB + b, :], start=(s == 0 and b == 0),
                                           stop=(s == NS - 1 and b == GB - 1))
                else:
                    pe.wait_ge(s_basis, g + 1 - ON_PE)
                    for b in range(GB):
                        mm = pe.matmul(bank[g][:, b * D:(b + 1) * D], basis[:, g, b * P:(b + 1) * P],
                                       amps[:, g * GB + b, :], start=True, stop=True)
                mm.then_inc(s_field, 1)

            def turn(n, g):
                pe.wait_ge(s_normed[n], g + 1)
                if n == 0 and g:
                    pe.wait_ge(s_drive, g)
                if n == 1 and g:
                    pe.wait_ge(s_H, KH * g)
                for c in range(2):
                    mm = pe.transpose(turn_bank[n][:, c * P:(c + 1) * P],
                                      normed[n][:, g, 2 * c:2 * c + 2, :].rearrange("p b d -> p (b d)"), identity)
                mm.then_inc(s_turn[n], 1)

            def inputs_in(g):
                if g == 0:
                    pe.wait_ge(ld["state"], 16)
                pe.wait_ge(s_xT[0], g + 1)
                for h in range(2):
                    mm = pe.matmul(state_bank[:, h * 2 * P:(h + 1) * 2 * P], B_rows[h],
                                   xT[:, g].rearrange("p b t -> p (b t)"), start=True, stop=True)
                mm.then_inc(s_v, 1)

            def outputs(g):
                if g == 0:
                    pe.wait_ge(s_tables, 1)
                pe.wait_ge(s_turned, g + 1)
                if g:
                    pe.wait_ge(s_hb, g)
                for j in range(GB):
                    b = 2 * (j % 2) + j // 2
                    for r, c in ((0, C_re), (1, neg_C_im[:, :])):
                        mm = pe.matmul(layer_bank[:, b * D:(b + 1) * D], turned[:, g, r, j * P:(j + 1) * P], c,
                                       start=(r == 0), stop=(r == 1))
                mm.then_inc(s_y, 1)

            def hidden(g):
                pe.wait_ge(s_xT[1], g + 1)
                if g:
                    pe.wait_ge(s_lread, g)
                for k in range(KH):
                    for h in range(2):
                        rows = slice(h * D, (h + 1) * D)
                        mm = pe.matmul(hid_pair[:, h, k * 2 * P:(k + 1) * 2 * P], W1[rows, k * P:(k + 1) * P],
                                       x2T[rows, g].rearrange("p b t -> p (b t)"), start=True, stop=True)
                mm.then_inc(s_hid, 1)

            def gate(g):
                pe.wait_ge(s_H, KH * (g + 1))
                for j in range(GB):
                    for k in range(KH):
                        mm = pe.matmul(logit_bank[:, j * NE:(j + 1) * NE], H[:, g, k, j * P:(j + 1) * P], Wg[:, k, :],
                                       start=(k == 0), stop=(k == KH - 1))
                mm.then_inc(s_logit, 1)

            def experts(g, h):
                pe.wait_ge(s_H, KH * (g + 1))
                if g == 0:
                    pe.wait_ge(ld["wd"], 16)
                    pe.wait_ge(s_bd_split, 3)
                if g == 0:
                    pe.wait_ge(s_ha, 2 * h + 2)
                if g:
                    pe.wait_ge(s_copied[h], NE * g)
                for jj in range(2):
                    j = 2 * h + jj
                    for k in range(KH):
                        pe.matmul(pair[h][:, jj, :], H[:, g, k, j * P:(j + 1) * P], wd_sb[:, k, :],
                                  start=(k == 0), stop=False)
                    mm = pe.matmul(pair[h][:, jj, :], ones[:, :], bdp[:, :], start=False, stop=True)
                mm.then_inc(s_exp_mm[h], 1)

            keep_warm(16)
            field(0)
            field(1)
            keep_warm(6)
            turn(0, 0)
            inputs_in(0)
            keep_warm(14)
            outputs(0)
            field(2)
            turn(0, 1)
            inputs_in(1)
            turn(1, 0)
            hidden(0)
            outputs(1)
            field(3)
            experts(0, 0)
            turn(0, 2)
            turn(1, 1)
            gate(0)
            inputs_in(2)
            experts(0, 1)
            turn(0, 3)
            hidden(1)
            inputs_in(3)
            outputs(2)
            experts(1, 1)
            gate(1)
            turn(1, 2)
            outputs(3)
            hidden(2)
            experts(1, 0)
            gate(2)
            turn(1, 3)
            experts(2, 1)
            hidden(3)
            experts(2, 0)
            gate(3)
            experts(3, 1)
            experts(3, 0)




def _pack(table, width, **parts):
    out = np.zeros((P, width), np.float32)
    for name, a in parts.items():
        out[0:a.shape[0], table[name]] = a.reshape(a.shape[0], -1)
    return out


def _rows(a):
    return np.broadcast_to(a.reshape(1, -1), (P, a.size))


def kernel(x, fside_BS_continuous_positions, L0_tok_emb, L0_tok_locality_shapes, L0_tok_w1, L0_tok_b1,
           L0_tok_w2, L0_tok_b2, L0_tok_w3, L0_tok_b3, L0_tok_multiscale_widths, L0_tok_scale_weights,
           L0_attn_log_lambda_real, L0_attn_lambda_imag, L0_attn_log_dt, L0_attn_B, L0_attn_C_real,
           L0_attn_C_imag, L0_ffn_W1, L0_ffn_b1, L0_ffn_Wg, L0_ffn_bg, L0_ffn_Wd, L0_ffn_bd):
    import concourse.bacc as bacc
    from concourse.bass_utils import run_bass_kernel_spmd

    a = {k: np.asarray(v) for k, v in locals().items() if k[0:3] in ("L0_", "fsi") or k == "x"}
    twice = lambda v: np.concatenate([v, v], axis=0)

    line = np.arange(P)
    shift = np.zeros((P, P + 2), np.float32)
    shift[line, line + 1] = 1
    w3 = a["L0_tok_w3"][0]
    w3_both = np.zeros((2, D, 2, K3), np.float32)
    w3_both[0, :, 0], w3_both[1, :, 1] = w3, w3
    small = _pack(
        SMALL, NSMALL, shift=shift,
        half0=(line < D).astype(np.float32)[:, None], half1=(line >= D).astype(np.float32)[:, None],
        value=(line % V).astype(np.float32)[:, None],
        place=(line.astype(np.float32) / np.float32(P - 1))[:, None],
        emb=np.concatenate([a["L0_tok_emb"], a["L0_tok_locality_shapes"]], axis=1),
        b1=a["L0_tok_b1"][:, None], b2=twice(a["L0_tok_b2"])[:, None], b3=_rows(a["L0_tok_b3"]),
        widths=_rows(a["L0_tok_multiscale_widths"]), weights=_rows(a["L0_tok_scale_weights"]),
        log_re=twice(a["L0_attn_log_lambda_real"])[:, None], im=twice(a["L0_attn_lambda_imag"])[:, None],
        log_dt=twice(a["L0_attn_log_dt"])[:, None], w3=w3_both.reshape(2 * D, 2 * K3),
        ffn_b1=a["L0_ffn_b1"].reshape(KH, P).T, bg=_rows(a["L0_ffn_bg"]))
    w1 = np.zeros((2, V, 4, C1), np.float32)
    for k in range(K1):
        w1[k % 2, :, k // 2, :] = a["L0_tok_w1"][:, :, k].T
    w2 = a["L0_tok_w2"].transpose(1, 2, 0)
    B_rows = np.zeros((2, D, 2, P), np.float32)
    for h in range(2):
        B_rows[h, :, h, :] = np.concatenate([a["L0_attn_B"].T] * 2, axis=1)
    state = _pack(
        STATE, NSTATE, B=B_rows.reshape(P, 2 * P), C_re=twice(a["L0_attn_C_real"].T),
        C_im=twice(a["L0_attn_C_imag"].T), W1=twice(a["L0_ffn_W1"]),
        Wg=a["L0_ffn_Wg"].reshape(KH, P, NE).transpose(1, 0, 2))
    wd = a["L0_ffn_Wd"].reshape(NE, KH, P, D).transpose(2, 1, 0, 3).reshape(P, KH, NE * D)
    bd = np.zeros((96, NE * D), np.float32)
    bd[0], bd[32], bd[64] = (a["L0_ffn_bd"].reshape(-1),) * 3

    arrays = {"x": a["x"], "positions": a["fside_BS_continuous_positions"], "small": small,
              "w1": w1.reshape(P, 4, C1), "w2": w2, "state": state, "wd": wd, "bd": bd}
    arrays = {k: np.ascontiguousarray(v) for k, v in arrays.items()}

    nc = bacc.Bacc("TRN2", target_bir_lowering=False, num_devices=1)
    ins = [nc.dram_tensor(n, v.shape, mybir.dt.from_np(v.dtype), kind="ExternalInput").ap()
           for n, v in arrays.items()]
    out = nc.dram_tensor("out", (NB, P, D), F32, kind="ExternalOutput").ap()
    tower(nc, *ins, out)
    r = run_bass_kernel_spmd(nc, [arrays], core_ids=[0])
    return r.results[0]["out"]
```

```python
from contextlib import ExitStack

import concourse.bass as bass
import numpy as np
from concourse import mybir

ALU = mybir.AluOpType
ACT = mybir.ActivationFunctionType
F32 = mybir.dt.float32
BF16 = mybir.dt.bfloat16
F32R = mybir.dt.float32r
I32 = mybir.dt.int32

P = 128
NB = 16
G = 4
GB = NB // G
T = GB * P
D = 64
V = 64
NL = 4
NS = 4
C1 = 128
K1, K2, K3 = 7, 5, 3
HID = 256
KH = HID // P
NE = 8
PADX = P + 6
PADH = P + 4
TURN = 2.0 ** 26
TURN_MASK = 0x3FFFFFC
PI_BELOW = 3.1415925
EPS = 1e-5
ROUND = 1.5 * 2.0 ** 23


def columns(*parts):
    at, out = 0, {}
    for name, width in parts:
        out[name] = slice(at, at + width)
        at += width
    return out, at


SMALL, NSMALL = columns(
    ("shift", P + 2), ("half0", 1), ("half1", 1), ("value", 1), ("place", 1), ("emb", D + NL),
    ("b1", 1), ("b2", 1), ("b3", 1), ("widths", NS), ("weights", NS),
    ("log_re", 1), ("im", 1), ("log_dt", 1), ("w3", 2 * K3), ("ffn_b1", KH), ("bg", NE))
STATE, NSTATE = columns(("B", 2 * P), ("C_re", D), ("C_im", D), ("W1", HID), ("Wg", KH * NE))


def repeat(ap, axis, n):
    ap = ap.unsqueeze(axis)
    shape = list(ap.shape)
    shape[axis] = n
    return ap.broadcast_to(shape)


def tower(nc, x, positions, small, w1, w2, state, wd, bd, out):
    ctx = ExitStack()
    with ctx:
        def sb(name, shape, dt=F32):
            return ctx.enter_context(nc.sbuf_tensor(name, shape, dt))

        def sem(name):
            return ctx.enter_context(nc.semaphore(name))

        pair = [ctx.enter_context(nc.psum_tensor(f"pair{i}", [P, 2, T], F32)) for i in range(2)]
        bank = [pair[i // 2][:, i % 2, :] for i in range(4)]
        bank += [ctx.enter_context(nc.psum_tensor(f"bank{i}", [P, T], F32))[:, :] for i in range(4, 6)]
        state_bank, layer_bank = bank[4], bank[5]
        hid_pair = ctx.enter_context(nc.psum_tensor("hid_pair", [P, 2, T], F32))
        bank += [hid_pair[:, i, :] for i in range(2)]
        turn_bank = (state_bank[:, 0:2 * P], bank[7][:, 0:2 * P])
        logit_bank = bank[6]

        sm = sb("sm", [P, NSMALL])
        w1_sb = sb("w1_sb", [P, 4, C1])
        w2_sb = sb("w2_sb", [P, K2, D])
        st_sb = sb("st_sb", [P, NSTATE])
        wd_sb = sb("wd_sb", [P, KH, NE * D])
        bd_sb = sb("bd_sb", [96, NE * D])
        posb = sb("posb", [P, NB, P])
        bytes_pad = sb("bytes_pad", [P, NB, PADX], I32)

        def col(name):
            return sm[:, SMALL[name]]

        identity = sm[:, SMALL["shift"].start + 1:SMALL["shift"].start + 1 + P]

        def shift(k):
            return sm[:, SMALL["shift"].start + k:SMALL["shift"].start + k + P]

        B_rows = [st_sb[:, STATE["B"].start + h * P:STATE["B"].start + (h + 1) * P] for h in range(2)]
        C_re = st_sb[:, STATE["C_re"]]
        W1 = st_sb[:, STATE["W1"]]
        Wg = st_sb[:, STATE["Wg"]].rearrange("p (k e) -> p k e", k=KH)

        embp = [sb(f"embp{i}", [V, D + NL], BF16) for i in range(3)]
        embr = [sb(f"embr{i}", [V, D + NL]) for i in range(2)]
        bdp = sb("bdp", [96, NE * D], BF16)
        bdh = [sb(f"bdh{i}", [96, NE * D], BF16) for i in range(3)]
        ones = sb("ones", [96, P], BF16)
        shapes = sb("shapes", [P, NB, NL])
        taps = sb("taps", [P, NB, K3])
        neg_b3 = sb("neg_b3", [P, 1])
        ctx_exp = sb("ctx_exp", [P, NB])
        amp_exp = sb("amp_exp", [P, NB])
        amp_tmp = sb("amp_tmp", [P, 3, NB])
        gain = sb("gain", [P, NB])
        amps = sb("amps", [P, NB, D])
        center = sb("center", [P, NB])
        absw = sb("absw", [P, NB])
        inv_width = sb("inv_width", [P, G, NS, GB])
        width = sb("width", [P, G, NS, GB])
        phase_tmp = sb("phase_tmp", [P, 3, NB])
        phase = sb("phase", [P, G, NS, GB])
        scale_w = sb("scale_w", [P, NS])
        dist = sb("dist", [P, NB, P])
        picked = sb("picked", [P, G, GB, D])
        wave = sb("wave", [P, G, NS * T])
        angle = sb("angle", [P, G, NS * T], I32)
        bell = sb("bell", [P, G, NS * T])
        bdr = [bell[0:96, G - 1, k * NE * D:(k + 1) * NE * D] for k in (1, 2)]
        basis = sb("basis", [P, G, T])
        neg_pi = sb("neg_pi", [P, 1])
        unused = sb("unused", [P, 1])
        minus_half = sb("minus_half", [P, NB])

        h_a = sb("h_a", [P, G, GB, D])
        h_b = sb("h_b", [P, G, GB, D])
        stats = sb("stats", [P, 2, G, GB, 6])
        mean_var = sb("mean_var", [P, 2, G, GB, 2])
        var_eps = sb("var_eps", [P, 2, G, GB])
        negated = sb("negated", [P, 2, G, GB])
        rstd = sb("rstd", [P, 2, G, GB])
        offset = sb("offset", [P, 2, G, GB])
        turned = wave[:, :, 0:2 * T].rearrange("p g (r t) -> p g r t", r=2)
        drive = wave[:, :, 2 * T:3 * T]
        modes = wave[:, :, 3 * T:4 * T]
        spent = angle[:, :, :].bitcast(F32)
        W = GB * D

        def spent_rows(k):
            return spent[:, :, k * W:(k + 1) * W].rearrange("p g (b d) -> p g b d", b=GB)

        normed = [spent_rows(0), spent_rows(1)]
        xT, x2T = (spent[:, :, k * W:(k + 1) * W].rearrange("p g (b t) -> p g b t", b=2) for k in (2, 3))
        scaled, result = spent_rows(4), spent_rows(5)
        H = bell[:, :, 0:KH * T].rearrange("p g (k t) -> p g k t", k=KH)
        neg_C_im = sb("neg_C_im", [P, D])
        spar = sb("spar", [P, 32])
        powers = sb("powers", [P, 2, P + 1])
        ptmp = sb("ptmp", [P, 4, P])
        drive_tab = sb("drive_tab", [P, P])
        turn_tab = sb("turn_tab", [P, 2, P])
        decay = sb("decay", [P, GB, P])
        logits = sb("logits", [P, G, GB, NE])
        top = sb("top", [P, G, GB])
        below = sb("below", [P, G, GB, NE])
        chosen = sb("chosen", [P, G, GB, NE], I32)
        expl = sb("expl", [P, G, GB, NE])
        denom = sb("denom", [P, G, GB])
        prob = sb("prob", [P, G, GB])

        with ExitStack() as early:
            def early_sb(name, shape, dt=F32):
                return early.enter_context(nc.sbuf_tensor(name, shape, dt))

            onehot = early_sb("onehot", [P, NB, PADX], F32R)
            onehot_b = early_sb("onehot_b", [V, NB, P], BF16)
            w1p = [early_sb(f"w1p{i}", [P, 4, C1], F32R) for i in range(2)]
            h1 = early_sb("h1", [P, NB, PADH])
            h2 = early_sb("h2", [P, G // 2, GB, P])
        wd_high, wd_low = (sb(f"wd_{n}", [P, KH, NE * D], F32R) for n in ("high", "low"))
        H_high, H_low = (sb(f"H_{n}", [P, 2, KH, T], F32R) for n in ("high", "low"))

        ld = {n: sem(f"ld_{n}") for n in ("x", "pos", "small", "w1", "w2", "state", "wd", "bd")}
        stored = sem("stored")
        dve_chain, pool_chain = sem("dve_chain"), sem("pool_chain")
        s_pad = sem("s_pad")
        s_cst = sem("s_cst")
        s_emb_split = sem("s_emb_split")
        s_onehot = sem("s_onehot")
        s_w1_part = sem("s_w1_part")
        s_bd_part, s_bd_left = sem("s_bd_part"), sem("s_bd_left")
        s_dist, s_picked0 = sem("s_dist"), sem("s_picked0")
        s_copied = [sem("s_copied0"), sem("s_copied1")]
        s_bd_split = sem("s_bd_split")
        s_shapes_mm, s_shapes, s_emb_mm = sem("s_shapes_mm"), sem("s_shapes"), sem("s_emb_mm")
        s_conv1, s_h1 = sem("s_conv1"), sem("s_h1")
        s_conv2, s_h2 = sem("s_conv2"), sem("s_h2")
        s_taps_mm, s_taps = sem("s_taps_mm"), sem("s_taps")
        s_ctx_mm, s_ctx = sem("s_ctx_mm"), sem("s_ctx")
        s_amp_exp, s_negb3 = sem("s_amp_exp"), sem("s_negb3")
        s_gain, s_amps = sem("s_gain"), sem("s_amps")
        s_phase, s_ampden = sem("s_phase"), sem("s_ampden")
        s_z, s_z_pool, s_angle = sem("s_z"), sem("s_z_pool"), sem("s_angle")
        s_square, s_square_pool, s_bell, s_cos = sem("s_square"), sem("s_square_pool"), sem("s_bell"), sem("s_cos")
        s_prod, s_basis, s_basis_pool = sem("s_prod"), sem("s_basis"), sem("s_basis_pool")
        s_sexp = sem("s_sexp")
        s_neg_C = sem("s_neg_C")
        s_tables = sem("s_tables")
        s_field, s_ha = sem("s_field"), sem("s_ha")
        s_mv = [sem("s_mv0"), sem("s_mv1")]
        s_rstd = [sem("s_rstd0"), sem("s_rstd1")]
        s_normed = [sem("s_normed0"), sem("s_normed1")]
        s_turn = [sem("s_turn0"), sem("s_turn1")]
        s_xT = [sem("s_xT0"), sem("s_xT1")]
        s_v, s_drive = sem("s_v"), sem("s_drive")
        s_turned = sem("s_turned")
        s_y, s_hb = sem("s_y"), sem("s_hb")
        s_wd_split, s_H_split = sem("s_wd_split"), sem("s_H_split")
        s_hid, s_H = sem("s_hid"), sem("s_H")
        s_logit, s_lread, s_below = sem("s_logit"), sem("s_lread"), sem("s_below")
        s_expl, s_prob = sem("s_expl"), sem("s_prob")
        s_exp_mm = [sem("s_exp_mm0"), sem("s_exp_mm1")]
        s_last_mm, s_last_copied = sem("s_last_mm"), sem("s_last_copied")
        s_result, s_last = sem("s_result"), sem("s_last")

        scale_pairs = [slice(k * T, (k + 2) * T) for k in range(0, NS, 2)]

        def widths_away(engine, g):
            return engine.tensor_tensor(
                wave[:, g, :].rearrange("p (s t) -> p s t", s=NS),
                repeat(dist[:, g * GB:(g + 1) * GB, :].rearrange("p b t -> p (b t)"), 1, NS),
                repeat(inv_width[:, g, :, :].rearrange("p s b -> p (s b)"), 2, P), ALU.mult)

        def z_is_there(engine, g):
            if g < G - 1:
                engine.wait_ge(s_z, g + 1)
            else:
                engine.wait_ge(s_z_pool, 1)

        block = ctx.enter_context(nc.Block())

        @block.sync
        def _(sp):
            sp.dma_start(sm[:, :], small).then_inc(ld["small"], 16)
            for half in range(2):
                rows = slice(half * V, half * V + V)
                sp.dma_start(bytes_pad[rows, :, 3 - half:3 - half + P], repeat(x, 0, V)).then_inc(ld["x"], 16)
            sp.dma_start(posb[:, :, :], repeat(positions, 0, P)).then_inc(ld["pos"], 16)
            sp.dma_start(w2_sb[:, :, :], w2).then_inc(ld["w2"], 16)
            sp.dma_start(st_sb[:, :], state).then_inc(ld["state"], 16)
            sp.dma_start(wd_sb[:, :, :], wd).then_inc(ld["wd"], 16)
            for g in range(G):
                if g < G - 1:
                    sp.wait_ge(s_result, g + 1)
                else:
                    sp.wait_ge(s_last, GB)
                sp.dma_start(out[g * GB:(g + 1) * GB].rearrange("b p d -> p b d"),
                             result[:, g]).then_inc(stored, 16)
            sp.wait_ge(stored, 16 * G)

        @block.gpsimd
        def _(pool):
            count = [0]

            def link(ins):
                count[0] += 1
                ins.then_inc(pool_chain, 1)
                pool.wait_ge(pool_chain, count[0])

            for half in range(2):
                rows = slice(half * V, half * V + V)
                for cols in (slice(0, 3 - half), slice(3 - half + P, PADX)):
                    pool.memset(bytes_pad[rows, :, cols], -1).then_inc(s_pad, 1)
                    pool.wait_ge(s_pad, 1 + 2 * half + (cols.start > 0))
            pool.memset(neg_pi[:, :], -PI_BELOW)
            pool.memset(h1[:, :, 0:2], 0.0)
            pool.memset(h1[:, :, 2 + P:], 0.0)
            pool.memset(ones[:, :], 1.0).then_inc(s_cst, 1)

            pool.memset(picked[:, :, :, :], 0.0).then_inc(s_picked0, 1)

            link(pool.memset(decay[:, :, :], 1.0))
            pool.memset(decay[:, :, 0:1], 0.0)
            link(pool.memset(minus_half[:, :], -0.5))
            slot = iter(range(32))

            def new():
                k = next(slot)
                return spar[:, k:k + 1]

            lam, dt = new(), new()
            pool.wait_ge(s_sexp, 2)
            dtc, hr, hi = new(), new(), new()
            link(pool.tensor_scalar(dtc, dt, 0.005, 0.1, ALU.max, ALU.min))
            link(pool.tensor_tensor(hr, dtc, lam, ALU.mult))
            link(pool.tensor_scalar(hr, hr, -0.5, None, ALU.mult))
            link(pool.tensor_tensor(hi, dtc, col("im"), ALU.mult))
            link(pool.tensor_scalar(hi, hi, 0.5, None, ALU.mult))
            low, high, hi2, d2, n2, inv = new(), new(), new(), new(), new(), new()
            link(pool.tensor_scalar(low, hr, -1.0, 1.0, ALU.mult, ALU.add))
            link(pool.tensor_scalar(high, hr, 1.0, None, ALU.add))
            link(pool.tensor_tensor(hi2, hi, hi, ALU.mult))
            link(pool.tensor_tensor(d2, low, low, ALU.mult))
            link(pool.tensor_tensor(d2, d2, hi2, ALU.add))
            link(pool.tensor_tensor(n2, high, high, ALU.mult))
            link(pool.tensor_tensor(n2, n2, hi2, ALU.add))
            link(pool.tensor_tensor(inv, d2, minus_half[:, 0:1], ALU.pow))
            link(pool.tensor_tensor(inv, inv, inv, ALU.mult))
            rho2, rho, irho, zero = new(), new(), new(), new()
            link(pool.tensor_tensor(rho2, n2, inv, ALU.mult))
            link(pool.tensor_scalar(zero, rho2, 1e-30, None, ALU.is_lt))
            link(pool.tensor_scalar(rho, rho2, 1e-30, None, ALU.max))
            link(pool.tensor_tensor(irho, rho, minus_half[:, 0:1], ALU.pow))
            link(pool.tensor_tensor(rho, rho2, irho, ALU.mult))
            link(pool.tensor_tensor(irho, irho, inv, ALU.mult))
            keep, c1, s1 = new(), new(), new()
            link(pool.tensor_scalar(keep, zero, -1.0, 1.0, ALU.mult, ALU.add))
            link(pool.tensor_tensor(irho, irho, keep, ALU.mult))
            link(pool.tensor_tensor(c1, low, high, ALU.mult))
            link(pool.tensor_tensor(c1, c1, hi2, ALU.subtract))
            link(pool.tensor_tensor(c1, c1, irho, ALU.mult))
            link(pool.tensor_tensor(powers[:, 0, 1:2], c1, zero, ALU.add))
            link(pool.tensor_scalar(s1, hi, 2.0, None, ALU.mult))
            link(pool.tensor_tensor(powers[:, 1, 1:2], s1, irho, ALU.mult))
            link(pool.memset(powers[:, 0, 0:1], 1.0))
            link(pool.memset(powers[:, 1, 0:1], 0.0))
            m = 1
            while m < P:
                c, s = powers[:, 0, m:m + 1], powers[:, 1, m:m + 1]
                link(pool.tensor_scalar(ptmp[:, 0:2, 0:m], powers[:, :, 1:m + 1], c, None, ALU.mult))
                link(pool.tensor_scalar(ptmp[:, 2:4, 0:m], powers[:, :, 1:m + 1], s, None, ALU.mult))
                link(pool.tensor_tensor(powers[:, 0, m + 1:2 * m + 1], ptmp[:, 0, 0:m], ptmp[:, 3, 0:m],
                                        ALU.subtract))
                link(pool.tensor_tensor(powers[:, 1, m + 1:2 * m + 1], ptmp[:, 1, 0:m], ptmp[:, 2, 0:m],
                                        ALU.add))
                m *= 2
            pool.wait_ge(s_dist, 1)
            widths_away(pool, G - 1).then_inc(s_z_pool, 1)
            pool.wait_ge(s_z, 3)
            pool.tensor_tensor(bell[:, 2, :], wave[:, 2, :], wave[:, 2, :], ALU.mult).then_inc(s_square_pool, 1)
            b_re, b_im, mix_c, mix_s, t0 = new(), new(), new(), new(), new()
            link(pool.tensor_tensor(t0, dtc, inv, ALU.mult))
            link(pool.tensor_tensor(b_re, t0, low, ALU.mult))
            link(pool.tensor_tensor(b_im, t0, hi, ALU.mult))
            link(pool.tensor_tensor(mix_c, b_re, col("half0"), ALU.mult))
            link(pool.tensor_tensor(t0, b_im, col("half1"), ALU.mult))
            link(pool.tensor_tensor(mix_c, mix_c, t0, ALU.add))
            link(pool.tensor_tensor(mix_s, b_im, col("half0"), ALU.mult))
            link(pool.tensor_tensor(t0, b_re, col("half1"), ALU.mult))
            link(pool.tensor_tensor(mix_s, mix_s, t0, ALU.subtract))
            cos_t, sin_t = powers[:, 0, 0:P], powers[:, 1, 0:P]
            link(pool.tensor_scalar(ptmp[:, 0, :], cos_t, mix_c, None, ALU.mult))
            link(pool.tensor_scalar(ptmp[:, 1, :], sin_t, mix_s, None, ALU.mult))
            link(pool.tensor_tensor(drive_tab[:, :], ptmp[:, 0, :], ptmp[:, 1, :], ALU.add))

            def last_tables():
                link(pool.tensor_scalar(ptmp[:, 0, :], cos_t, col("half0"), None, ALU.mult))
                link(pool.tensor_scalar(ptmp[:, 1, :], sin_t, col("half1"), None, ALU.mult))
                link(pool.tensor_tensor(turn_tab[:, 0, :], ptmp[:, 0, :], ptmp[:, 1, :], ALU.subtract))
                link(pool.tensor_scalar(ptmp[:, 2, :], sin_t, col("half0"), None, ALU.mult))
                link(pool.tensor_scalar(ptmp[:, 3, :], cos_t, col("half1"), None, ALU.mult))
                link(pool.tensor_tensor(turn_tab[:, 1, :], ptmp[:, 2, :], ptmp[:, 3, :], ALU.add))
                pool.tensor_scalar(decay[:, :, :], decay[:, :, :], rho, None, ALU.mult).then_inc(s_tables, 1)

            def sum_scales(g):
                pool.wait_ge(s_prod, NS * (g + 1))
                w = bell[:, g, :].rearrange("p (s t) -> p s t", s=NS)
                link(pool.tensor_tensor(w[:, 0:2, :], w[:, 0:2, :], w[:, 2:4, :], ALU.add))
                pool.tensor_tensor(basis[:, g, :], w[:, 0, :], w[:, 1, :], ALU.add).then_inc(s_basis_pool, 1)

            def inv_std(n, g):
                pool.wait_ge(s_mv[n], g + 1)
                link(pool.tensor_scalar(var_eps[:, n, g, :], mean_var[:, n, g, :, 1], EPS, None, ALU.add))
                pool.tensor_scalar(negated[:, n, g, :], mean_var[:, n, g, :, 0], -1.0, None, ALU.mult)
                link(pool.tensor_tensor(rstd[:, n, g, :], var_eps[:, n, g, :], minus_half[:, 0:GB], ALU.pow))
                pool.tensor_tensor(offset[:, n, g, :], negated[:, n, g, :], rstd[:, n, g, :],
                                   ALU.mult).then_inc(s_rstd[n], 1)

            def finish(g):
                if g == 0:
                    pool.wait_ge(s_prob, 1)
                for h in range(2):
                    pool.wait_ge(s_copied[h], NE * (g + 1))
                link(pool.tensor_tensor(
                    scaled[:, g].rearrange("p (b h) d -> p b h d", h=2),
                    picked[:, g].rearrange("p (b h) d -> p b h d", h=2),
                    repeat(prob[:, g].rearrange("p (h b) -> p b h", h=2), 3, D), ALU.mult))
                pool.tensor_tensor(result[:, g], scaled[:, g], h_b[:, g], ALU.add).then_inc(s_result, 1)

            last_tables()
            inv_std(0, 0)
            inv_std(0, 1)
            sum_scales(2)
            inv_std(1, 0)
            sum_scales(3)
            inv_std(0, 2)
            inv_std(1, 1)
            inv_std(0, 3)
            inv_std(1, 2)
            inv_std(1, 3)
            for g in range(G - 1):
                finish(g)

        @block.scalar
        def _(act):
            act.dma_start(w1_sb[:, :, :], w1).then_inc(ld["w1"], 16)
            act.dma_start(bd_sb[:, :], bd).then_inc(ld["bd"], 16)
            act.wait_ge(ld["small"], 16)
            act.activation(spar[:, 0:1], col("log_re"), ACT.Exp).then_inc(s_sexp, 1)
            act.activation(spar[:, 1:2], col("log_dt"), ACT.Exp).then_inc(s_sexp, 1)
            act.activation(neg_b3[:, :], col("b3"), ACT.Copy, scale=-1.0).then_inc(s_negb3, 1)
            act.wait_ge(ld["bd"], 16)
            act.copy(bdh[0][:], bd_sb[:]).then_inc(s_bd_part, 1)
            act.wait_ge(s_bd_left, 1)
            act.copy(bdh[1][:], bdr[0]).then_inc(s_bd_part, 1)
            act.wait_ge(s_shapes_mm, 1)
            act.copy(shapes[:, :, :].rearrange("p b c -> p (b c)"), bank[4][:, 0:NB * NL]).then_inc(s_shapes, 1)
            act.wait_ge(s_shapes, 1)
            act.activation(amp_exp[:, :], shapes[:, :, 2], ACT.Exp, scale=-1.0).then_inc(s_amp_exp, 1)
            act.wait_ge(ld["state"], 16)
            act.activation(neg_C_im[:, :], st_sb[:, STATE["C_im"]], ACT.Copy, scale=-1.0).then_inc(s_neg_C, 1)
            act.wait_ge(s_bd_left, 2)
            act.copy(bdh[2][:], bdr[1]).then_inc(s_bd_part, 1)

            def conv1_out(g):
                act.wait_ge(s_conv1, g + 1)
                act.activation(h1[:, g * GB:(g + 1) * GB, 2:2 + P],
                               bank[g].rearrange("p (b s) -> p b s", b=GB), ACT.Gelu,
                               bias=col("b1")).then_inc(s_h1, 1)

            def square(g):
                z_is_there(act, g)
                act.activation(bell[:, g, :], wave[:, g, :], ACT.Square).then_inc(s_square, 1)

            def load_gelu():
                act.activation(unused[:, :], neg_pi[:, :], ACT.Gelu)

            def square_is_there(g):
                if g == 2:
                    act.wait_ge(s_square_pool, 1)
                else:
                    act.wait_ge(s_square, min(g + 1, G - 1))

            def gaussian(g):
                square_is_there(g)
                act.activation(bell[:, g, :], bell[:, g, :], ACT.Exp, scale=-0.5).then_inc(s_bell, 1)

            def cosine(g):
                act.wait_ge(s_angle, g + 1)
                square_is_there(g)
                for part in scale_pairs:
                    act.activation(wave[:, g, part], angle[:, g, part], ACT.Sin, bias=neg_pi[:, 0:1],
                                   scale=2.0 * PI_BELOW / TURN).then_inc(s_cos, 1)

            act.wait_ge(s_cst, 1)
            conv1_out(0)
            square(0)
            conv1_out(1)
            conv1_out(2)
            square(1)
            conv1_out(3)
            for q in range(G // 2):
                act.wait_ge(s_conv2, q + 1)
                act.activation(h2[:, q, :, :].rearrange("p b s -> p (b s)"), bank[2 * q], ACT.Gelu,
                               bias=col("b2")).then_inc(s_h2, 1)
            gaussian(0)
            act.wait_ge(s_taps_mm, 1)
            act.copy(taps[:, :, :].rearrange("p b k -> p (b k)"), bank[1][:, 0:NB * K3]).then_inc(s_taps, 1)
            gaussian(1)
            act.wait_ge(s_ctx_mm, 1)
            act.wait_ge(s_negb3, 1)
            act.activation(ctx_exp[:, :], bank[3][:, 0:NB], ACT.Exp, bias=neg_b3[:, 0:1],
                           scale=-1.0).then_inc(s_ctx, 1)
            cosine(0)
            cosine(1)

            def field_out(g):
                act.wait_ge(s_field, g + 1)
                act.copy(h_a[:, g, :, :].rearrange("p b d -> p (b d)"), bank[g][:, 0:GB * D]).then_inc(s_ha, 1)

            def transposed_out(n, g):
                act.wait_ge(s_turn[n], g + 1)
                act.copy((xT, x2T)[n][:, g].rearrange("p b t -> p (b t)"), turn_bank[n]).then_inc(s_xT[n], 1)

            def normalise(n, g):
                act.wait_ge(s_rstd[n], g + 1)
                for b in range(GB):
                    ins = act.activation(normed[n][:, g, b, :], (h_a, h_b)[n][:, g, b, :], ACT.Identity,
                                         scale=rstd[:, n, g, b:b + 1], bias=offset[:, n, g, b:b + 1])
                ins.then_inc(s_normed[n], 1)

            def hidden(g):
                act.wait_ge(s_hid, g + 1)
                for k in range(KH):
                    act.activation(H[:, g, k, :].rearrange("p (h t) -> p h t", h=2),
                                   hid_pair[:, :, k * 2 * P:(k + 1) * 2 * P], ACT.Gelu,
                                   bias=sm[:, SMALL["ffn_b1"].start + k:SMALL["ffn_b1"].start + k + 1]).then_inc(s_H, 1)

            gaussian(2)
            square(3)
            gaussian(3)
            field_out(0)
            cosine(2)
            normalise(0, 0)
            field_out(1)
            transposed_out(0, 0)
            cosine(3)
            load_gelu()
            normalise(0, 1)
            transposed_out(0, 1)
            normalise(1, 0)
            transposed_out(1, 0)
            field_out(2)
            hidden(0)
            normalise(0, 2)
            transposed_out(0, 2)
            normalise(1, 1)
            transposed_out(1, 1)
            field_out(3)
            hidden(1)
            normalise(0, 3)
            normalise(1, 2)
            transposed_out(0, 3)
            transposed_out(1, 2)
            hidden(2)
            normalise(1, 3)
            transposed_out(1, 3)
            hidden(3)
            act.wait_ge(s_below, G)
            act.activation(expl[:, :, :, :], below[:, :, :, :], ACT.Exp).then_inc(s_expl, 1)

        @block.vector
        def _(dve):
            count = [0]

            def link(ins):
                count[0] += 1
                ins.then_inc(dve_chain, 1)
                dve.wait_ge(dve_chain, count[0])

            dve.wait_ge(ld["small"], 16)
            table = sm[0:V, SMALL["emb"]]
            link(dve.tensor_copy(embp[0][:], table))
            link(dve.tensor_tensor(embr[0][:], table, embp[0][:], ALU.subtract))
            link(dve.tensor_copy(embp[1][:], embr[0][:]))
            link(dve.tensor_tensor(embr[1][:], embr[0][:], embp[1][:], ALU.subtract))
            dve.tensor_copy(embp[2][:], embr[1][:]).then_inc(s_emb_split, 1)
            link(dve.tensor_tensor(scale_w[:, :], col("weights"), col("weights"), ALU.mult))
            dve.wait_ge(ld["w1"], 16)
            dve.tensor_copy(w1p[0][:], w1_sb[:]).then_inc(s_w1_part, 1)
            dve.wait_ge(s_w1_part, 1)
            dve.tensor_tensor(w1p[1][:], w1_sb[:], w1p[0][:].bitcast(F32), ALU.subtract).then_inc(s_w1_part, 1)
            dve.wait_ge(s_pad, 4)
            dve.wait_ge(ld["x"], 32)
            dve.tensor_scalar(onehot_b[:, :, :], bytes_pad[0:V, :, 3:3 + P], sm[0:V, SMALL["value"]], None,
                              ALU.is_equal).then_inc(s_onehot, 1)
            dve.tensor_scalar(onehot[:, :, :], bytes_pad[:, :, :], col("value"), None,
                              ALU.is_equal).then_inc(s_onehot, 1)
            for k in range(2):
                dve.wait_ge(s_bd_part, k + 1)
                dve.tensor_tensor(bdr[k], bd_sb[:] if k == 0 else bdr[0], bdh[k][:],
                                  ALU.subtract).then_inc(s_bd_left, 1)
            dve.wait_ge(s_shapes, 1)
            lp = [shapes[:, :, k] for k in range(NL)]
            dve.tensor_scalar(center[:, :], lp[0], 0.05, col("place"), ALU.mult, ALU.add)
            dve.tensor_scalar(phase_tmp[:, 0, :], lp[3], 0.5, ROUND, ALU.mult, ALU.add)
            link(dve.scalar_tensor_tensor(out=absw[:, :], in0=lp[1], scalar=-1.0, in1=lp[1], op0=ALU.mult, op1=ALU.max))
            dve.tensor_scalar(phase_tmp[:, 1, :], phase_tmp[:, 0, :], -ROUND, None, ALU.add)
            for s in range(NS):
                c = SMALL["widths"].start + s
                ins = dve.tensor_scalar(width[:, :, s, :], absw[:, :].rearrange("p (g b) -> p g b", g=G),
                                        sm[:, c:c + 1], 1e-5, ALU.mult, ALU.add)
            link(ins)
            dve.scalar_tensor_tensor(out=phase_tmp[:, 2, :], in0=lp[3], scalar=0.5, in1=phase_tmp[:, 1, :],
                                     op0=ALU.mult, op1=ALU.subtract)
            link(dve.reciprocal(inv_width[:, :, :, :], width[:, :, :, :]))
            dve.tensor_scalar(phase[:, :, :, :],
                              repeat(phase_tmp[:, 2, :].rearrange("p (g b) -> p g b", g=G), 2, NS),
                              0.75, TURN, ALU.add, ALU.mult).then_inc(s_phase, 1)
            dve.wait_ge(ld["pos"], 16)
            dve.tensor_tensor(dist[:, :, :], posb[:, :, :], repeat(center[:, :], 2, P),
                              ALU.subtract).then_inc(s_dist, 1)
            dve.wait_ge(s_dist, 1)

            def z(g):
                widths_away(dve, g).then_inc(s_z, 1)

            def turns(g):
                z_is_there(dve, g)
                link(dve.scalar_tensor_tensor(
                    out=angle[:, g, :].rearrange("p (s t) -> p s t", t=P),
                    in0=wave[:, g, :].rearrange("p (s t) -> p s t", t=P), scalar=TURN,
                    in1=repeat(phase[:, g, :, :].rearrange("p s b -> p (s b)"), 2, P),
                    op0=ALU.mult, op1=ALU.add))
                dve.tensor_scalar(angle[:, g, :], angle[:, g, :], TURN_MASK, None,
                                  ALU.bitwise_and).then_inc(s_angle, 1)

            def biases():
                dve.wait_ge(s_bd_part, 3)
                for k in range(3):
                    ins = dve.tensor_copy(bdp[32 * k:32 * k + 32, :], bdh[k][32 * k:32 * k + 32, :])
                ins.then_inc(s_bd_split, 1)

            def split_weights():
                dve.wait_ge(ld["wd"], 16)
                dve.wait_ge(s_ctx_mm, 1)
                link(dve.tensor_copy(wd_high[:, :, :], wd_sb[:, :, :]))
                dve.tensor_tensor(wd_low[:, :, :], wd_sb[:, :, :], wd_high[:, :, :].bitcast(F32),
                                  ALU.subtract).then_inc(s_wd_split, 1)

            def split_hidden(g):
                if g > 1:
                    for h in range(2):
                        dve.wait_ge(s_exp_mm[h], g - 1)
                for k in range(KH):
                    dve.wait_ge(s_H, KH * g + k + 1)
                    link(dve.tensor_copy(H_high[:, g % 2, k, :], H[:, g, k, :]))
                    dve.tensor_tensor(H_low[:, g % 2, k, :], H[:, g, k, :], H_high[:, g % 2, k, :].bitcast(F32),
                                      ALU.subtract).then_inc(s_H_split, 1)

            def gates():
                dve.wait_ge(s_ctx, 1)
                dve.wait_ge(s_ampden, 1)
                for q in range(2):
                    cols = slice(8 * q, 8 * q + 8)
                    ins = dve.scalar_tensor_tensor(
                        out=amp_tmp[:, 1, cols].rearrange("p (r b) -> p r b", r=2),
                        in0=ctx_exp[:, cols].rearrange("p (b r) -> p r b", r=2), scalar=1.0,
                        in1=amp_tmp[:, 0, cols].rearrange("p (r b) -> p r b", r=2), op0=ALU.add, op1=ALU.mult)
                link(ins)
                dve.reciprocal(gain[:, :], amp_tmp[:, 1, :]).then_inc(s_gain, 1)
                dve.wait_ge(s_gain, 1)
                for q in range(2):
                    b = slice(8 * q, 8 * q + 8)
                    dve.wait_ge(s_emb_mm, q + 1)
                    dve.tensor_tensor(amps[:, b, :], bank[4 + q].rearrange("p (b d) -> p b d", d=D),
                                      repeat(gain[:, b], 2, D), ALU.mult).then_inc(s_amps, 1)

            def product(g):
                for s in range(NS):
                    if s % 2 == 0:
                        dve.wait_ge(s_cos, 2 * g + s // 2 + 1)
                    part = slice(s * T, (s + 1) * T)
                    dve.scalar_tensor_tensor(out=bell[:, g, part], in0=bell[:, g, part],
                                             scalar=scale_w[:, s:s + 1], in1=wave[:, g, part],
                                             op0=ALU.mult, op1=ALU.mult).then_inc(s_prod, 1)

            def sum_scales(g):
                dve.wait_ge(s_prod, NS * (g + 1))
                w = bell[:, g, :].rearrange("p (s t) -> p s t", s=NS)
                link(dve.tensor_tensor(w[:, 0:2, :], w[:, 0:2, :], w[:, 2:4, :], ALU.add))
                dve.tensor_tensor(basis[:, g, :], w[:, 0, :], w[:, 1, :], ALU.add).then_inc(s_basis, 1)

            def moments(n, g):
                if n == 0:
                    dve.wait_ge(s_ha, g + 1)
                for b in range(GB):
                    ins = dve.bn_stats(stats[:, n, g, b, :], (h_a, h_b)[n][:, g, b, :])
                link(ins)
                for b in range(GB):
                    ins = dve.bn_aggr(mean_var[:, n, g, b, :], stats[:, n, g, b, :])
                ins.then_inc(s_mv[n], 1)

            def recurrence(g):
                if g == 0:
                    dve.wait_ge(s_tables, 1)
                dve.wait_ge(s_v, g + 1)
                dve.tensor_tensor(drive[:, g, :].rearrange("p (b t) -> p b t", b=GB),
                                  state_bank.rearrange("p (b t) -> p b t", b=GB),
                                  repeat(drive_tab[:, :], 1, GB), ALU.mult).then_inc(s_drive, 1)
                dve.wait_ge(s_drive, g + 1)
                link(dve.tensor_tensor_scan(modes[:, g, :], decay[:, :, :].rearrange("p b t -> p (b t)"),
                                            drive[:, g, :], 0.0, ALU.mult, ALU.add))
                for r in range(2):
                    ins = dve.tensor_tensor(turned[:, g, r, :].rearrange("p (b t) -> p b t", b=GB),
                                            modes[:, g, :].rearrange("p (b t) -> p b t", b=GB),
                                            repeat(turn_tab[:, r, :], 1, GB), ALU.mult)
                ins.then_inc(s_turned, 1)

            def residual(g):
                dve.wait_ge(s_y, g + 1)
                dve.wait_ge(s_ha, g + 1)
                dve.tensor_tensor(h_b[:, g, :, :].rearrange("p b d -> p (b d)"),
                                  h_a[:, g, :, :].rearrange("p b d -> p (b d)"),
                                  layer_bank[:, 0:GB * D], ALU.add).then_inc(s_hb, 1)
                dve.wait_ge(s_hb, g + 1)
                moments(1, g)

            def route(g):
                dve.wait_ge(s_logit, g + 1)
                dve.tensor_tensor(logits[:, g, :, :], logit_bank[:, 0:GB * NE].rearrange("p (b e) -> p b e", b=GB),
                                  repeat(col("bg"), 1, GB), ALU.add).then_inc(s_lread, 1)
                dve.wait_ge(s_lread, g + 1)
                link(dve.tensor_reduce(top[:, g, :], logits[:, g, :, :], mybir.AxisListType.X, ALU.max))
                dve.tensor_tensor(below[:, g, :, :], logits[:, g, :, :],
                                  repeat(top[:, g, :], 2, NE), ALU.subtract).then_inc(s_below, 1)
                dve.wait_ge(s_below, g + 1)
                link(dve.tensor_scalar(chosen[:, g, :, :], below[:, g, :, :], 0.0, None, ALU.is_ge))

            def pick(g, h):
                if g == 0:
                    dve.wait_ge(s_picked0, 1)
                dve.wait_ge(s_exp_mm[h], g + 1)
                for e in reversed(range(NE)):
                    if e < NE - 1:
                        dve.wait_ge(s_copied[h], NE * g + NE - 1 - e)
                    dve.copy_predicated(
                        picked[:, g, :, :].rearrange("p (b h) d -> p h b d", h=2)[:, h],
                        repeat(chosen[:, g, 2 * h:2 * h + 2, e], 2, D),
                        pair[h][:, :, e * D:(e + 1) * D]).then_inc(s_copied[h], 1)

            def pick_last(jj):
                dve.wait_ge(s_last_mm, jj + 1)
                for e in reversed(range(NE)):
                    if e < NE - 1:
                        dve.wait_ge(s_last_copied, NE * jj + NE - 1 - e)
                    dve.copy_predicated(
                        picked[:, G - 1, 2 * jj + 1, :], repeat(chosen[:, G - 1, 2 + jj, e:e + 1], 2, D)[:, 0],
                        pair[1][:, jj, e * D:(e + 1) * D]).then_inc(s_last_copied, 1)

            def probability():
                dve.wait_ge(s_expl, 1)
                link(dve.tensor_reduce(denom[:, :, :].rearrange("p g b -> p (g b)"),
                                       expl[:, :, :, :].rearrange("p g b e -> p (g b) e"),
                                       mybir.AxisListType.X, ALU.add))
                dve.reciprocal(prob[:, :, :], denom[:, :, :]).then_inc(s_prob, 1)

            def finish_last(b):
                dve.scalar_tensor_tensor(
                    out=result[:, G - 1, b, :], in0=picked[:, G - 1, b, :],
                    scalar=prob[:, G - 1, 2 * (b % 2) + b // 2:2 * (b % 2) + b // 2 + 1],
                    in1=h_b[:, G - 1, b, :], op0=ALU.mult, op1=ALU.add).then_inc(s_last, 1)

            z(0)
            dve.wait_ge(s_phase, 1)
            turns(0)
            z(1)
            turns(1)
            z(2)
            turns(2)
            dve.wait_ge(s_amp_exp, 1)
            dve.tensor_scalar(amp_tmp[:, 0, :], amp_exp[:, :], 1.0, None, ALU.add).then_inc(s_ampden, 1)
            biases()
            turns(3)
            product(0)
            gates()
            sum_scales(0)
            product(1)
            moments(0, 0)
            sum_scales(1)
            product(2)
            moments(0, 1)
            recurrence(0)
            residual(0)
            product(3)
            recurrence(1)
            moments(0, 2)
            split_weights()
            split_hidden(0)
            residual(1)
            recurrence(2)
            route(0)
            moments(0, 3)
            residual(2)
            pick(0, 0)
            split_hidden(1)
            route(1)
            recurrence(3)
            pick(0, 1)
            residual(3)
            pick(1, 0)
            split_hidden(2)
            route(2)
            pick(1, 1)
            pick(2, 0)
            split_hidden(3)
            pick(2, 1)
            route(3)
            pick(3, 0)
            probability()
            dve.wait_ge(s_prob, 1)
            dve.wait_ge(s_copied[0], NE * G)
            finish_last(0)
            finish_last(2)
            for jj in range(2):
                pick_last(jj)
                dve.wait_ge(s_last_copied, NE * (jj + 1))
                finish_last(2 * jj + 1)

        @block.tensor
        def _(pe):
            def keep_warm(n, free):
                for _ in range(n):
                    pe.matmul(bank[free], w1p[0][:, 0, :], w1p[0][:].rearrange("p j c -> p (j c)"),
                              start=True, stop=True)

            pe.wait_ge(s_w1_part, 1)
            keep_warm(9, 7)
            pe.wait_ge(s_emb_split, 1)
            pe.wait_ge(s_onehot, 1)

            def look_up(where, b, cols):
                for part in range(3):
                    mm = pe.matmul(where, onehot_b[:, b, :], embp[part][:, cols],
                                   start=(part == 0), stop=(part == 2))
                return mm

            for b in range(NB):
                mm = look_up(bank[4][:, b * NL:(b + 1) * NL], b, slice(D, D + NL))
            mm.then_inc(s_shapes_mm, 1)
            pe.wait_ge(s_w1_part, 2)
            pe.wait_ge(s_onehot, 2)
            for g in range(G):
                n = 0
                for part in range(2):
                    for j in range(4):
                        mm = pe.matmul(bank[g], w1p[part][:, j, :],
                                       onehot[:, g * GB:(g + 1) * GB, 2 * j:2 * j + P],
                                       start=(n == 0), stop=(n == 7))
                        n += 1
                mm.then_inc(s_conv1, 1)
            pe.wait_ge(ld["w2"], 16)
            for q in range(G // 2):
                for r in range(2):
                    g = 2 * q + r
                    pe.wait_ge(s_h1, g + 1)
                    for k in range(K2):
                        mm = pe.matmul(bank[2 * q][r * D:(r + 1) * D, :], w2_sb[:, k, :],
                                       h1[:, g * GB:(g + 1) * GB, k:k + P],
                                       start=(k == 0), stop=(k == K2 - 1))
                mm.then_inc(s_conv2, 1)
            for q in range(G // 2):
                pe.wait_ge(s_h2, q + 1)
                for b in range(GB):
                    c = (q * GB + b) * 2 * K3
                    mm = pe.matmul(bank[1][:, c:c + 2 * K3], h2[:, q, b, :], col("w3"), start=True, stop=True)
            mm.then_inc(s_taps_mm, 1)
            pe.wait_ge(s_shapes, 1)
            for q in range(2):
                for b in range(8):
                    mm = look_up(bank[4 + q][:, b * D:(b + 1) * D], 8 * q + b, slice(0, D))
                mm.then_inc(s_emb_mm, 1)
            pe.wait_ge(s_taps, 1)
            for k in range(K3):
                mm = pe.matmul(bank[3][:, 0:NB], shift(k), taps[:, :, k],
                               start=(k == 0), stop=(k == K3 - 1))
            mm.then_inc(s_ctx_mm, 1)

            def field(g):
                pe.wait_ge(s_amps, g // 2 + 1)
                if g < 2:
                    pe.wait_ge(s_basis, g + 1)
                else:
                    pe.wait_ge(s_basis_pool, g - 1)
                for b in range(GB):
                    mm = pe.matmul(bank[g][:, b * D:(b + 1) * D], basis[:, g, b * P:(b + 1) * P],
                                   amps[:, g * GB + b, :], start=True, stop=True)
                mm.then_inc(s_field, 1)

            def turn(n, g):
                pe.wait_ge(s_normed[n], g + 1)
                if n == 0 and g:
                    pe.wait_ge(s_drive, g)
                if n == 1 and g:
                    pe.wait_ge(s_H, KH * g)
                for c in range(2):
                    mm = pe.transpose(turn_bank[n][:, c * P:(c + 1) * P],
                                      normed[n][:, g, 2 * c:2 * c + 2, :].rearrange("p b d -> p (b d)"), identity)
                mm.then_inc(s_turn[n], 1)

            def inputs_in(g):
                if g == 0:
                    pe.wait_ge(ld["state"], 16)
                pe.wait_ge(s_xT[0], g + 1)
                for h in range(2):
                    mm = pe.matmul(state_bank[:, h * 2 * P:(h + 1) * 2 * P], B_rows[h],
                                   xT[:, g].rearrange("p b t -> p (b t)"), start=True, stop=True)
                mm.then_inc(s_v, 1)

            def outputs(g):
                if g == 0:
                    pe.wait_ge(s_neg_C, 1)
                pe.wait_ge(s_turned, g + 1)
                if g:
                    pe.wait_ge(s_hb, g)
                for j in range(GB):
                    b = 2 * (j % 2) + j // 2
                    for r, c in ((0, C_re), (1, neg_C_im[:, :])):
                        mm = pe.matmul(layer_bank[:, b * D:(b + 1) * D], turned[:, g, r, j * P:(j + 1) * P], c,
                                       start=(r == 0), stop=(r == 1))
                mm.then_inc(s_y, 1)

            def hidden(g):
                pe.wait_ge(s_xT[1], g + 1)
                if g:
                    pe.wait_ge(s_lread, g)
                for k in range(KH):
                    for h in range(2):
                        rows = slice(h * D, (h + 1) * D)
                        mm = pe.matmul(hid_pair[:, h, k * 2 * P:(k + 1) * 2 * P], W1[rows, k * P:(k + 1) * P],
                                       x2T[rows, g].rearrange("p b t -> p (b t)"), start=True, stop=True)
                mm.then_inc(s_hid, 1)

            def gate(g):
                pe.wait_ge(s_H, KH * (g + 1))
                for j in range(GB):
                    for k in range(KH):
                        mm = pe.matmul(logit_bank[:, j * NE:(j + 1) * NE], H[:, g, k, j * P:(j + 1) * P], Wg[:, k, :],
                                       start=(k == 0), stop=(k == KH - 1))
                mm.then_inc(s_logit, 1)

            def experts(g, h):
                pe.wait_ge(s_H_split, KH * (g + 1))
                if g == 0:
                    pe.wait_ge(s_wd_split, 1)
                    pe.wait_ge(s_bd_split, 1)
                    pe.wait_ge(s_ha, 2 * h + 2)
                if g:
                    pe.wait_ge(s_copied[h], NE * g)
                for jj in range(2):
                    j = 2 * h + jj
                    for k in range(KH):
                        cols = slice(j * P, (j + 1) * P)
                        for n, (hidden_part, weights) in enumerate((
                                (H_high, wd_high), (H_high, wd_low), (H_low, wd_high))):
                            pe.matmul(pair[h][:, jj, :], hidden_part[:, g % 2, k, cols], weights[:, k, :],
                                      start=(k == 0 and n == 0), stop=False)
                    mm = pe.matmul(pair[h][:, jj, :], ones[:, :], bdp[:, :], start=False, stop=True)
                    if (g, h) == (G - 1, 1):
                        mm.then_inc(s_last_mm, 1)
                if (g, h) != (G - 1, 1):
                    mm.then_inc(s_exp_mm[h], 1)

            keep_warm(30, 7)
            field(0)
            keep_warm(21, 7)
            field(1)
            keep_warm(2, 7)
            turn(0, 0)
            keep_warm(2, 7)
            inputs_in(0)
            keep_warm(14, 7)
            outputs(0)
            turn(0, 1)
            keep_warm(3, 7)
            field(2)
            inputs_in(1)
            keep_warm(9, 7)
            turn(1, 0)
            keep_warm(2, 3)
            hidden(0)
            outputs(1)
            gate(0)
            turn(0, 2)
            field(3)
            inputs_in(2)
            experts(0, 0)
            turn(1, 1)
            outputs(2)
            hidden(1)
            experts(0, 1)
            turn(0, 3)
            gate(1)
            inputs_in(3)
            turn(1, 2)
            experts(1, 0)
            outputs(3)
            hidden(2)
            experts(1, 1)
            gate(2)
            turn(1, 3)
            experts(2, 0)
            hidden(3)
            experts(2, 1)
            gate(3)
            experts(3, 0)
            experts(3, 1)



def _pack(table, width, **parts):
    out = np.zeros((P, width), np.float32)
    for name, a in parts.items():
        out[0:a.shape[0], table[name]] = a.reshape(a.shape[0], -1)
    return out


def _rows(a):
    return np.broadcast_to(a.reshape(1, -1), (P, a.size))


def kernel(x, fside_BS_continuous_positions, L0_tok_emb, L0_tok_locality_shapes, L0_tok_w1, L0_tok_b1,
           L0_tok_w2, L0_tok_b2, L0_tok_w3, L0_tok_b3, L0_tok_multiscale_widths, L0_tok_scale_weights,
           L0_attn_log_lambda_real, L0_attn_lambda_imag, L0_attn_log_dt, L0_attn_B, L0_attn_C_real,
           L0_attn_C_imag, L0_ffn_W1, L0_ffn_b1, L0_ffn_Wg, L0_ffn_bg, L0_ffn_Wd, L0_ffn_bd):
    import concourse.bacc as bacc
    from concourse.bass_utils import run_bass_kernel_spmd

    a = {k: np.asarray(v) for k, v in locals().items() if k[0:3] in ("L0_", "fsi") or k == "x"}
    twice = lambda v: np.concatenate([v, v], axis=0)

    line = np.arange(P)
    shift = np.zeros((P, P + 2), np.float32)
    shift[line, line + 1] = 1
    w3 = a["L0_tok_w3"][0]
    w3_both = np.zeros((2, D, 2, K3), np.float32)
    w3_both[0, :, 0], w3_both[1, :, 1] = w3, w3
    small = _pack(
        SMALL, NSMALL, shift=shift,
        half0=(line < D).astype(np.float32)[:, None], half1=(line >= D).astype(np.float32)[:, None],
        value=(line % V).astype(np.float32)[:, None],
        place=(line.astype(np.float32) / np.float32(P - 1))[:, None],
        emb=np.concatenate([a["L0_tok_emb"], a["L0_tok_locality_shapes"]], axis=1),
        b1=a["L0_tok_b1"][:, None], b2=twice(a["L0_tok_b2"])[:, None], b3=_rows(a["L0_tok_b3"]),
        widths=_rows(a["L0_tok_multiscale_widths"]), weights=_rows(a["L0_tok_scale_weights"]),
        log_re=twice(a["L0_attn_log_lambda_real"])[:, None], im=twice(a["L0_attn_lambda_imag"])[:, None],
        log_dt=twice(a["L0_attn_log_dt"])[:, None], w3=w3_both.reshape(2 * D, 2 * K3),
        ffn_b1=a["L0_ffn_b1"].reshape(KH, P).T, bg=_rows(a["L0_ffn_bg"]))
    w1 = np.zeros((2, V, 4, C1), np.float32)
    for k in range(K1):
        w1[k % 2, :, k // 2, :] = a["L0_tok_w1"][:, :, k].T
    w2 = a["L0_tok_w2"].transpose(1, 2, 0)
    B_rows = np.zeros((2, D, 2, P), np.float32)
    for h in range(2):
        B_rows[h, :, h, :] = np.concatenate([a["L0_attn_B"].T] * 2, axis=1)
    state = _pack(
        STATE, NSTATE, B=B_rows.reshape(P, 2 * P), C_re=twice(a["L0_attn_C_real"].T),
        C_im=twice(a["L0_attn_C_imag"].T), W1=twice(a["L0_ffn_W1"]),
        Wg=a["L0_ffn_Wg"].reshape(KH, P, NE).transpose(1, 0, 2))
    wd = a["L0_ffn_Wd"].reshape(NE, KH, P, D).transpose(2, 1, 0, 3).reshape(P, KH, NE * D)
    bd = np.zeros((96, NE * D), np.float32)
    bd[0], bd[32], bd[64] = (a["L0_ffn_bd"].reshape(-1),) * 3

    arrays = {"x": a["x"], "positions": a["fside_BS_continuous_positions"], "small": small,
              "w1": w1.reshape(P, 4, C1), "w2": w2, "state": state, "wd": wd, "bd": bd}
    arrays = {k: np.ascontiguousarray(v) for k, v in arrays.items()}

    nc = bacc.Bacc("TRN2", target_bir_lowering=False, num_devices=1)
    ins = [nc.dram_tensor(n, v.shape, mybir.dt.from_np(v.dtype), kind="ExternalInput").ap()
           for n, v in arrays.items()]
    out = nc.dram_tensor("out", (NB, P, D), F32, kind="ExternalOutput").ap()
    tower(nc, *ins, out)
    r = run_bass_kernel_spmd(nc, [arrays], core_ids=[0])
    return r.results[0]["out"]
```
